# Optimizing a Trainium2 kernel written in Bass

```python
import numpy as np
import jax
import jax.numpy as jnp

def _softmax(x, axis=-1):
    return jax.nn.softmax(x, axis=axis)

def _gelu(x):
    return jax.nn.gelu(x, approximate=True)

def _silu(x):
    return jax.nn.silu(x)

def _sigmoid(x):
    return jax.nn.sigmoid(x)

def _layernorm(x, axis=-1, eps=1e-05):
    m = jnp.mean(x, axis=axis, keepdims=True)
    v = jnp.var(x, axis=axis, keepdims=True)
    return (x - m) / jnp.sqrt(v + eps)

def _scatter_add(tgt, idx, src, axis=0):
    return tgt.at[idx].add(src)

def _segment_sum(src, seg, n):
    return jax.ops.segment_sum(src, seg, n)
kernel_name = 'mk_seq_postln_d1_jaxref_r4_eefe30'

def setup_inputs(seed: int=0):
    np.random.seed(seed)
    _w = jnp.asarray

    def _L0_attn_setup():
        import jax, jax.numpy as jnp
        import numpy as np
        D_MODEL = 512
        NUM_HEADS = 16
        HEAD_DIM = D_MODEL // NUM_HEADS
        LAYER_IDX = 0
        NUM_LAYERS = 13
        REINIT_LAMBDA = 0.8

        def _heads(t, B, S):
            return t.reshape(B, S, NUM_HEADS, HEAD_DIM).transpose(0, 2, 1, 3)
        key = jax.random.key(seed)
        ks = jax.random.split(key, 8)
        B, S = (2, 512)
        x = jax.random.normal(ks[0], (B, S, D_MODEL), dtype=jnp.float32)
        init = 1.0 / np.sqrt(D_MODEL)

        def w(k):
            return jax.random.uniform(k, (D_MODEL, D_MODEL), dtype=jnp.float32, minval=-init, maxval=init)
        lam_init = REINIT_LAMBDA * ((LAYER_IDX + 1) / NUM_LAYERS)
        return {'x': x, 'q1_w': w(ks[1]), 'k1_w': w(ks[2]), 'q2_w': w(ks[3]), 'k2_w': w(ks[4]), 'v_w': w(ks[5]), 'o_w': w(ks[6]), 'lambda_param': jnp.full((NUM_HEADS,), lam_init, dtype=jnp.float32)}
    _L0_attn_in = _L0_attn_setup()

    def _L0_ffn_setup():
        import jax, jax.numpy as jnp
        import numpy as np
        D_MODEL = 512
        HIDDEN = int(2 * D_MODEL * 4 / 3)

        def ternary_quant(w):
            s = jnp.mean(jnp.abs(w))
            q = jnp.clip(jnp.round(w / s), -1.0, 1.0) * s
            return w + jax.lax.stop_gradient(q - w)
        key = jax.random.key(seed)
        k0, k1, k2, k3 = jax.random.split(key, 4)
        x = jax.random.normal(k0, (4, 1024, D_MODEL), dtype=jnp.float32)
        std_in = 1.0 / np.sqrt(D_MODEL)
        std_h = 1.0 / np.sqrt(HIDDEN)
        w1 = jax.random.uniform(k1, (HIDDEN, D_MODEL), jnp.float32, -std_in, std_in)
        w3 = jax.random.uniform(k2, (HIDDEN, D_MODEL), jnp.float32, -std_in, std_in)
        w2 = jax.random.uniform(k3, (D_MODEL, HIDDEN), jnp.float32, -std_h, std_h)
        return {'x': x, 'w1': w1, 'w3': w3, 'w2': w2}
    _L0_ffn_in = _L0_ffn_setup()
    _d = {'L0_attn_x': _L0_attn_in['x'], 'L0_attn_q1_w': _L0_attn_in['q1_w'], 'L0_attn_k1_w': _L0_attn_in['k1_w'], 'L0_attn_q2_w': _L0_attn_in['q2_w'], 'L0_attn_k2_w': _L0_attn_in['k2_w'], 'L0_attn_v_w': _L0_attn_in['v_w'], 'L0_attn_o_w': _L0_attn_in['o_w'], 'L0_attn_lambda_param': _L0_attn_in['lambda_param'], 'L0_ffn_w1': _L0_ffn_in['w1'], 'L0_ffn_w3': _L0_ffn_in['w3'], 'L0_ffn_w2': _L0_ffn_in['w2']}
    _x0 = _d['L0_attn_x']
    _d['L0_attn_x'] = jax.random.normal(jax.random.fold_in(jax.random.key(seed), 1), (2, 1024, 512), dtype=_x0.dtype)
    del _x0
    return _d

def reference(L0_attn_x, L0_attn_q1_w, L0_attn_k1_w, L0_attn_q2_w, L0_attn_k2_w, L0_attn_v_w, L0_attn_o_w, L0_attn_lambda_param, L0_ffn_w1, L0_ffn_w3, L0_ffn_w2):

    def _L0_attn_ref(x, q1_w, k1_w, q2_w, k2_w, v_w, o_w, lambda_param):
        import jax, jax.numpy as jnp
        import numpy as np
        D_MODEL = 512
        NUM_HEADS = 16
        HEAD_DIM = D_MODEL // NUM_HEADS
        LAYER_IDX = 0
        NUM_LAYERS = 13
        REINIT_LAMBDA = 0.8

        def _heads(t, B, S):
            return t.reshape(B, S, NUM_HEADS, HEAD_DIM).transpose(0, 2, 1, 3)
        B, S, _ = x.shape
        q1 = _heads(x @ q1_w.T, B, S)
        k1 = _heads(x @ k1_w.T, B, S)
        q2 = _heads(x @ q2_w.T, B, S)
        k2 = _heads(x @ k2_w.T, B, S)
        v = _heads(x @ v_w.T, B, S)
        scale = jnp.sqrt(jnp.float32(HEAD_DIM))
        attn1 = jax.nn.softmax(jnp.einsum('bhqd,bhkd->bhqk', q1, k1) / scale, axis=-1)
        attn2 = jax.nn.softmax(jnp.einsum('bhqd,bhkd->bhqk', q2, k2) / scale, axis=-1)
        lam = lambda_param.reshape(1, NUM_HEADS, 1, 1)
        out = jnp.einsum('bhqk,bhkd->bhqd', attn1 - lam * attn2, v)
        out = out.transpose(0, 2, 1, 3).reshape(B, S, D_MODEL)
        return out @ o_w.T

    def _L0_ffn_ref(x, w1, w3, w2):
        import jax, jax.numpy as jnp
        import numpy as np
        D_MODEL = 512
        HIDDEN = int(2 * D_MODEL * 4 / 3)

        def ternary_quant(w):
            s = jnp.mean(jnp.abs(w))
            q = jnp.clip(jnp.round(w / s), -1.0, 1.0) * s
            return w + jax.lax.stop_gradient(q - w)
        w1q = ternary_quant(w1)
        w3q = ternary_quant(w3)
        w2q = ternary_quant(w2)
        h1 = jnp.einsum('bsd,hd->bsh', x, w1q)
        h3 = jnp.einsum('bsd,hd->bsh', x, w3q)
        g = jax.nn.silu(h1) * h3
        return jnp.einsum('bsh,dh->bsd', g, w2q)
    x = L0_attn_x
    x = _layernorm(x + _L0_attn_ref(x, L0_attn_q1_w, L0_attn_k1_w, L0_attn_q2_w, L0_attn_k2_w, L0_attn_v_w, L0_attn_o_w, L0_attn_lambda_param), axis=-1)
    x = _layernorm(x + _L0_ffn_ref(x, L0_ffn_w1, L0_ffn_w3, L0_ffn_w2), axis=-1)
    return x

_drawn_inputs = setup_inputs


def setup_inputs(seed=0):
    import zlib

    import numpy as np

    out = dict(_drawn_inputs(seed))
    spreads = {'L0_attn_lambda_param': (0.0615384615957737, 0.6)}
    factors = {'L0_attn_q1_w': 8.0,
     'L0_attn_k1_w': 7.967,
     'L0_attn_q2_w': 8.0,
     'L0_attn_k2_w': 8.0,
     'L0_attn_v_w': 4.791,
     'L0_attn_o_w': 4.723}
    for name, (base, spread) in spreads.items():
        noise = np.random.default_rng([zlib.crc32(name.encode()), seed]).standard_normal(out[name].shape)
        drawn = base * np.exp(spread * noise) if base else spread * noise
        out[name] = jnp.asarray(drawn.astype(out[name].dtype))
    for name, factor in factors.items():
        out[name] = (out[name] * factor).astype(out[name].dtype)
    return out
```

```python
from contextlib import ExitStack

import concourse.bass as bass
from concourse import mybir

F32 = mybir.dt.float32
F32R = mybir.dt.float32r
F16 = mybir.dt.float16
ALU = mybir.AluOpType
ACT = mybir.ActivationFunctionType
AX = mybir.AxisListType

P = 128
B, S, D = 2, 1024, 512
H, DH = 16, 32
HIDDEN = int(2 * D * 4 / 3)
T = B * S
KC = D // P
FC = -(-HIDDEN // P)
HP = FC * P
LAST = HIDDEN - (FC - 1) * P
G = P // DH
NG = H // G
QB = 512
NQB = S // QB
SC = S // P
HALF = 256
HT = HALF // P
NH2 = QB // HALF
UNITS = NH2 * G * HT
NGRP = B * NQB * NG
MATS = 4
EPS = 1e-5
SCORE_SCALE = float(DH) ** -0.5
XSCALE = 1024.0
GSCALE = 2.0 ** -24


def ternary_weights(nc, ctx, w1T, w3T, w2T, w13, w2, facs):
    sb, sem = scopes(nc, ctx)
    raw = sb("q_raw", [P, 3, FC * D], F32)
    tmp = sb("q_tmp", [P, HP * KC], F16)
    part = sb("q_part", [P, 3], F32)
    total = sb("q_total", [P, 3], F32)
    half = sb("q_half", [P, 6], F32)
    prod = sb("q_prod", [P, 1], F32)
    zeroed, loaded, summed, reduced, step, done = (sem(n) for n in ("q_zeroed", "q_loaded", "q_summed",
                                                                   "q_reduced", "q_step", "q_done"))
    r1, r3 = (raw[:, m, 0:KC * HIDDEN].rearrange("p (c f) -> p c f", c=KC) for m in (0, 1))
    r2 = raw[:, 2, :].rearrange("p (c d) -> p c d", c=FC)
    with nc.Block() as block:
        @block.sync
        def _(sp):
            sp.dma_start(r1, w1T.rearrange("(c p) f -> p c f", p=P)).then_inc(loaded, 16)
            sp.dma_start(r3, w3T.rearrange("(c p) f -> p c f", p=P)).then_inc(loaded, 16)
            sp.wait_ge(zeroed, 1)
            sp.dma_start(r2[:, 0:FC - 1, :], w2T[0:(FC - 1) * P, :].rearrange("(c p) d -> p c d", p=P)).then_inc(loaded, 16)
            sp.dma_start(r2[0:LAST, FC - 1, :], w2T[(FC - 1) * P:HIDDEN, :]).then_inc(loaded, 16)

        @block.gpsimd
        def _(pool):
            nc.gpsimd.memset(r2[:, FC - 1, :], 0.0).then_inc(zeroed, 1)
            pool.wait_ge(summed, 3)
            nc.gpsimd.partition_all_reduce(total[:], part[:], P, bass.bass_isa.ReduceOp.add).then_inc(reduced, 1)

        @block.vector
        def _(dve):
            dve.wait_ge(loaded, 64)
            for m, r in enumerate((r1, r3, r2)):
                nc.vector.tensor_reduce(part[:, m:m + 1], r, axis=AX.XY, op=ALU.add,
                                        apply_absolute_value=True).then_inc(summed, 1)
            dve.wait_ge(reduced, 1)
            inv = 1.0 / (HIDDEN * D)
            nc.vector.tensor_scalar(half[:, 0:3], total[:], inv * 0.5, None, ALU.mult).then_inc(step, 1)
            nc.vector.tensor_scalar(half[:, 3:6], total[:], inv * -0.5, None, ALU.mult).then_inc(step, 1)
            dve.wait_ge(step, 2)
            nc.vector.tensor_scalar(facs[:, 0:1], half[:, 0:1], 1.0 / XSCALE, None, ALU.mult).then_inc(step, 1)
            nc.vector.tensor_tensor(prod[:], half[:, 0:1], half[:, 1:2], ALU.mult).then_inc(step, 1)
            dve.wait_ge(step, 4)
            nc.vector.tensor_scalar(facs[:, 1:2], prod[:], half[:, 2:3], 4.0 / (XSCALE * XSCALE * GSCALE),
                                    ALU.mult, ALU.mult).then_inc(done, 1)
            t = tmp[:, 0:KC * HIDDEN].rearrange("p (c f) -> p c f", c=KC)
            t2 = tmp[:, 0:FC * D].rearrange("p (c d) -> p c d", c=FC)
            n = 4
            for m in (0, 1):
                nc.vector.memset(w13[:, m, :, HIDDEN:HP], 0.0).then_inc(done, 1)
            for m, r, below, out in ((0, r1, t, w13[:, 0, :, 0:HIDDEN]), (1, r3, t, w13[:, 1, :, 0:HIDDEN]),
                                     (2, r2, t2, w2[:])):
                nc.vector.tensor_scalar(below, r, half[:, 3 + m:4 + m], None, ALU.is_lt).then_inc(step, 1)
                n += 1
                dve.wait_ge(step, n)
                nc.vector.scalar_tensor_tensor(out, r, half[:, m:m + 1], below, ALU.is_gt,
                                               ALU.subtract).then_inc(step, 1)
                n += 1
                dve.wait_ge(step, n)


def scopes(nc, ctx):
    def sb(name, shape, dt):
        return ctx.enter_context(nc.sbuf_tensor(name, shape, dt))

    def sem(name):
        return ctx.enter_context(nc.semaphore(name))
    return sb, sem


def projections(nc, ctx, xT, wT, qk, vs, psum):
    sb, sem = scopes(nc, ctx)
    NW = 5
    w_raw = sb("p_w_raw", [P, 2, KC * D], F32)
    w_hi = sb("p_w_hi", [P, NW, KC, D], F32R)
    w_lo = sb("p_w_lo", [P, NW, KC, D], F32R)
    x_raw = sb("p_x_raw", [P, KC, S], F32)
    x_hi = sb("p_x_hi", [P, KC, S], F32R)
    x_lo = sb("p_x_lo", [P, KC, S], F32R)
    out_hi = sb("p_out_hi", [P, 2, D], F32R)
    out_lo = sb("p_out_lo", [P, 2, D], F32R)
    out_v = sb("p_out_v", [P, 2, D], F32)
    w_in = [sem(f"p_w_in{i}") for i in range(2)]
    x_in, w_split_hi, w_split_lo, x_split_hi, x_split_lo, product, got_hi, got_lo = (sem(n) for n in (
        "p_x_in", "p_w_split_hi", "p_w_split_lo", "p_x_split_hi", "p_x_split_lo", "p_product", "p_got_hi", "p_got_lo"))
    stored = [sem(f"p_stored{i}") for i in range(2)]
    NB = 4
    jobs = [("qk", m, mt, tb) for tb in range(S // D) for m in range(MATS) for mt in range(KC)]
    jobs += [("v", 0, 0, tt) for tt in range(SC)]
    NJ = len(jobs)

    with nc.Block() as block:
        @block.sync
        def _(sp):
            for w in range(NW):
                if w >= 2:
                    sp.wait_ge(w_split_lo, w - 1)
                sp.dma_start(w_raw[:, w % 2, :].rearrange("p (c d) -> p c d", c=KC),
                             wT[w].rearrange("(c p) d -> p c d", p=P)).then_inc(w_in[w % 2], 16)
            with sp.Fori(0, B) as b:
                sp.wait_ge(x_split_lo, b * KC)
                sp.dma_start(x_raw[:], xT[bass.ds(b, 1)].rearrange("a (c p) t -> p (a c) t", p=P)).then_inc(x_in, 16)
                for j, (kind, m, mt, tb) in enumerate(jobs):
                    sp.wait_ge(got_lo, b * NJ + j + 1)
                    if kind == "qk":
                        for part, stage in ((0, out_hi), (1, out_lo)):
                            dst = qk[bass.ds(b, 1), m, part, mt * P:(mt + 1) * P, tb * D:(tb + 1) * D]
                            sp.dma_start(dst.rearrange("a f t -> f (a t)"),
                                         stage[:, j % 2, :].bitcast(F32)).then_inc(stored[j % 2], 16)
                    else:
                        for c in range(2):
                            dst = vs[bass.ds(b, 1), tb * P:(tb + 1) * P, c * HALF:(c + 1) * HALF]
                            sp.dma_start(dst.rearrange("a t f -> t (a f)"),
                                         out_v[:, j % 2, c * HALF:(c + 1) * HALF]).then_inc(stored[j % 2], 16)
            for i in range(2):
                sp.wait_ge(stored[i], B * NJ // 2 * 32)

        @block.scalar
        def _(act):
            for w in range(NW):
                act.wait_ge(w_in[w % 2], 16 * (w // 2 + 1))
                nc.scalar.activation(w_hi[:, w].rearrange("p c d -> p (c d)"), w_raw[:, w % 2, :],
                                     ACT.Copy).then_inc(w_split_hi, 1)
            with act.Fori(0, B) as b:
                act.wait_ge(x_in, b * 16 + 16)
                act.wait_ge(product, b * NJ)
                for c in range(KC):
                    nc.scalar.activation(x_hi[:, c, :], x_raw[:, c, :], ACT.Copy).then_inc(x_split_hi, 1)
                for j, (kind, m, mt, tb) in enumerate(jobs):
                    act.wait_ge(product, b * NJ + j + 1)
                    act.wait_ge(stored[j % 2], b * (NJ // 2 * 32) + j // 2 * 32)
                    if kind == "v":
                        nc.scalar.activation(out_v[:, j % 2, 0:HALF], psum[:, j % NB, 0:HALF], ACT.Copy).then_inc(got_hi, 1)
                    else:
                        nc.scalar.activation(out_hi[:, j % 2, :], psum[:, j % NB, :], ACT.Copy,
                                             scale=SCORE_SCALE if m % 2 == 0 else 1.0).then_inc(got_hi, 1)

        @block.vector
        def _(dve):
            for w in range(NW):
                dve.wait_ge(w_split_hi, w + 1)
                nc.vector.tensor_tensor(w_lo[:, w].rearrange("p c d -> p (c d)"), w_raw[:, w % 2, :],
                                        w_hi[:, w].rearrange("p c d -> p (c d)").bitcast(F32), ALU.subtract).then_inc(w_split_lo, 1)
            with dve.Fori(0, B) as b:
                dve.wait_ge(product, b * NJ)
                for c in range(KC):
                    dve.wait_ge(x_split_hi, b * KC + c + 1)
                    nc.vector.tensor_tensor(x_lo[:, c, :], x_raw[:, c, :], x_hi[:, c, :].bitcast(F32),
                                            ALU.subtract).then_inc(x_split_lo, 1)
                for j, (kind, m, mt, tb) in enumerate(jobs):
                    dve.wait_ge(got_hi, b * NJ + j + 1)
                    if kind == "v":
                        nc.vector.tensor_copy(out_v[:, j % 2, HALF:D], psum[:, j % NB, HALF:D]).then_inc(got_lo, 1)
                    else:
                        nc.vector.scalar_tensor_tensor(out_lo[:, j % 2, :], psum[:, j % NB, :],
                                                       SCORE_SCALE if m % 2 == 0 else 1.0,
                                                       out_hi[:, j % 2, :].bitcast(F32), ALU.mult, ALU.subtract).then_inc(got_lo, 1)

        @block.tensor
        def _(pe):
            pe.wait_ge(w_split_lo, NW)
            with pe.Fori(0, B) as b:
                for j, (kind, m, mt, tb) in enumerate(jobs):
                    if j == 0:
                        pe.wait_ge(x_split_lo, b * KC + KC)
                    if j >= NB:
                        pe.wait_ge(got_lo, b * NJ + j - NB + 1)
                    else:
                        pe.wait_ge(got_lo, b * NJ)
                    n = 0
                    for xp, wp in ((x_hi, w_hi), (x_hi, w_lo), (x_lo, w_hi)):
                        for c in range(KC):
                            if kind == "qk":
                                lhsT, rhs = wp[:, m, c, mt * P:(mt + 1) * P], xp[:, c, tb * D:(tb + 1) * D]
                            else:
                                lhsT, rhs = xp[:, c, tb * P:(tb + 1) * P], wp[:, MATS, c, :]
                            last = nc.tensor.matmul(psum[:, j % NB, :], lhsT, rhs, start=n == 0, stop=n == 3 * KC - 1)
                            n += 1
                    last.then_inc(product, 1)


def attention(nc, ctx, lam, qk, vs, oT, ident, psum):
    sb, sem = scopes(nc, ctx)
    k_st = sb("k_st", [3 * DH, G, 2, S], F32R)
    q_st = sb("q_st", [3 * DH, G, 2, QB], F32R)
    v_st = sb("v_st", [P, SC, P], F32)
    e = sb("e", [P, 2, 2, S], F32)
    mix = sb("mix", [P, 2, S], F32)
    mixT = sb("mixT", [P, NH2, SC, G, HALF], F32)
    nmax = sb("nmax", [P, 2, 2], F32)
    sums = sb("sums", [P, UNITS, 2], F32)
    rsum = sb("rsum", [P, UNITS, 2], F32)
    coef = sb("coef", [P, UNITS], F32)
    ratio = sb("ratio", [P, UNITS], F32)
    ones = sb("ones", [P, P], F32)
    nlam = sb("nlam", [P, NGRP * G], F32)
    nlam4 = sb("nlam4", [P, G], F32)
    lam_raw = sb("lam_raw", [P, H], F32)
    rep = sb("rep", [P, HT, G, DH], F32)
    rT = sb("rT", [P, HALF], F32)
    o_out = sb("o_out", [P, 2, HALF], F32)

    score_bank = [psum[:, 2 * a:2 * a + 2, :] for a in range(2)]
    flip_bank = [psum[:, 4 + i, :] for i in range(2)]
    pv_bank = psum[:, 6, 0:HALF]
    r_bank = psum[:, 7, 0:HALF]

    stack_in = [sem(f"a_stack_in{h}") for h in range(G)]
    scored = [sem(f"a_scored{a}") for a in range(2)]
    maxed = [sem(f"a_maxed{a}") for a in range(2)]
    exped = [sem(f"a_exped{a}") for a in range(2)]
    v_in, inverted, weighted, combined, flipped, evacuated, pv_done, rep_ready, rep_flipped, rT_ready, o_ready, lam_in, lam_step = (
        sem("a_" + n) for n in ("v_in", "inverted", "weighted", "combined", "flipped", "evacuated", "pv_done", "rep_ready",
                                "rep_flipped", "rT_ready", "o_ready", "lam_in", "lam_step"))
    stored = [sem(f"a_stored{i}") for i in range(2)]
    divided = sem("a_divided")

    def unit(u):
        half, rest = divmod(u, G * HT)
        return half, rest // HT, rest % HT

    def load_stacks(sp, i, h):
        b, tb, g = i // (NQB * NG), (i // NG) % NQB, i % NG
        for a in range(2):
            for slot, part in enumerate((0, 0, 1)):
                src = qk[bass.ds(b, 1), 2 * a, part, bass.ds(g * P + h * DH, DH), bass.ds(tb * QB, QB)]
                sp.dma_start(q_st[slot * DH:(slot + 1) * DH, h, a, :].bitcast(F32),
                             src.rearrange("a f t -> f (a t)")).then_inc(stack_in[h], 16)
            for slot, part in enumerate((0, 1, 0)):
                src = qk[bass.ds(b, 1), 2 * a + 1, part, bass.ds(g * P + h * DH, DH), :]
                sp.dma_start(k_st[slot * DH:(slot + 1) * DH, h, a, :].bitcast(F32),
                             src.rearrange("a f t -> f (a t)")).then_inc(stack_in[h], 16)

    def store_out(sp, i, half):
        sp.wait_ge(o_ready, 2 * i + half + 1)
        dst = oT[bass.ds((i % NG) * P, P), bass.ds((i // NG) * QB + half * HALF, HALF)]
        sp.dma_start(dst, o_out[:, half, :]).then_inc(stored[half], 16)

    def load_v(sp, i):
        sp.wait_ge(pv_done, 2 * i)
        b, g = i // (NQB * NG), i % NG
        sp.dma_start(v_st[:], vs[bass.ds(b, 1), :, bass.ds(g * P, P)].rearrange("a (c p) f -> p (a c) f", p=P)).then_inc(v_in, 16)

    with nc.Block() as block:
        @block.sync
        def _(sp):
            sp.dma_start(lam_raw[:], lam.partition_broadcast(P)).then_inc(lam_in, 16)
            for h in range(G):
                load_stacks(sp, 0, h)
            with sp.Fori(0, NGRP - 1) as i:
                load_v(sp, i)
                for h in range(G):
                    sp.wait_ge(scored[1], UNITS * i + UNITS // 2 + HT * (h + 1))
                    load_stacks(sp, i + 1, h)
                    if h == 1:
                        store_out(sp, i, 0)
                store_out(sp, i, 1)
            load_v(sp, NGRP - 1)
            store_out(sp, NGRP - 1, 0)
            store_out(sp, NGRP - 1, 1)
            for half in range(2):
                sp.wait_ge(stored[half], 16 * NGRP)

        @block.gpsimd
        def _(pool):
            pool.wait_ge(lam_in, 16)
            for r in range(NGRP * G // H):
                nc.gpsimd.tensor_scalar(nlam[:, r * H:(r + 1) * H], lam_raw[:], -1.0, 1.0, ALU.mult, ALU.mult).then_inc(lam_step, 1)
            nc.gpsimd.memset(ones[:], 1.0).then_inc(lam_step, 1)
            base = NGRP * G // H + 1
            pool.wait_ge(lam_step, base)
            with pool.Fori(0, NGRP) as i:
                pool.wait_ge(weighted, UNITS * i)
                nc.gpsimd.tensor_tensor(nlam4[:], nlam[:, bass.ds(i * G, G)], ones[:, 0:G], ALU.mult).then_inc(lam_step, 1)
                pool.wait_ge(lam_step, i + base + 1)
                for u in range(UNITS):
                    half, h, qt = unit(u)
                    pool.wait_ge(inverted, UNITS * i + u + 1)
                    nc.gpsimd.tensor_tensor(ratio[:, u:u + 1], sums[:, u, 0:1], rsum[:, u, 1:2], ALU.mult).then_inc(divided, 1)
                    pool.wait_ge(divided, UNITS * i + u + 1)
                    nc.gpsimd.tensor_tensor(coef[:, u:u + 1], ratio[:, u:u + 1], nlam4[:, h:h + 1], ALU.mult).then_inc(weighted, 1)
                    if u % (UNITS // 2) == UNITS // 2 - 1:
                        pool.wait_ge(rep_flipped, 2 * i + half)
                        src = rsum[:, half * G * HT:(half + 1) * G * HT, 0].rearrange("p (h q) -> p h q", h=G)
                        for q in range(HT):
                            last = nc.gpsimd.tensor_tensor(rep[:, q], src[:, :, q].unsqueeze(2).to_broadcast([P, G, DH]),
                                                           ones[:].rearrange("p (h d) -> p h d", d=DH), ALU.mult)
                        last.then_inc(rep_ready, 1)

        def act_unit(act, i, u, first):
            half, h, qt = unit(u)
            n = UNITS * i + u
            for a in range(2):
                act.wait_ge(maxed[a], n + 1)
                if not (first and u < 2):
                    act.wait_ge(combined, n - 1)
                nc.scalar.activation(e[:, a, u % 2, :], score_bank[a].rearrange("p b k -> p (b k)"), ACT.Exp,
                                     bias=nmax[:, a, u % 2:u % 2 + 1],
                                     accum_out=sums[:, u, a:a + 1]).then_inc(exped[a], 1)

        def act_evacuate(act, i, u, first):
            if first and u < 2:
                return
            m = (u - 2) % UNITS
            half, h, qt = unit(m)
            n = UNITS * i + u - 2
            if m % (UNITS // 2) == 0 and not first:
                act.wait_ge(pv_done, 2 * i + half - 1)
            for t in range(2):
                act.wait_ge(flipped, 2 * n + t + 1)
                nc.scalar.activation(mixT[:, half, t * 4:t * 4 + 4, h, qt * P:(qt + 1) * P],
                                     flip_bank[t].rearrange("p (c q) -> p c q", q=P), ACT.Copy).then_inc(evacuated, 1)

        def act_half(act, hn):
            act.wait_ge(rep_flipped, hn + 1)
            act.wait_ge(o_ready, hn)
            nc.scalar.activation(rT[:], r_bank, ACT.Copy).then_inc(rT_ready, 1)

        @block.scalar
        def _(act):
            def step(i, first):
                for u in range(UNITS):
                    act_unit(act, i, u, first)
                    act_evacuate(act, i, u, first)
                    if u == 3 and not first:
                        act_half(act, 2 * i - 1)
                    if u == 3 + UNITS // 2:
                        act_half(act, 2 * i)
            step(0, True)
            with act.Fori(1, NGRP) as i:
                step(i, False)
            for u in range(2):
                act_evacuate(act, NGRP, u, False)
            act_half(act, 2 * NGRP - 1)

        def combine(dve, i, u, first):
            if first and u == 0:
                return
            m = (u - 1) % UNITS
            n = UNITS * i + u - 1
            dve.wait_ge(weighted, n + 1)
            if not (first and u < 3):
                dve.wait_ge(flipped, 2 * (n - 1))
            nc.vector.scalar_tensor_tensor(mix[:, m % 2, :], e[:, 1, m % 2, :], coef[:, m:m + 1], e[:, 0, m % 2, :],
                                           ALU.mult, ALU.add).then_inc(combined, 1)

        def invert(dve, i, u, first):
            if first and u == 0:
                return
            m = (u - 1) % UNITS
            for a in range(2):
                dve.wait_ge(exped[a], UNITS * i + u)
            nc.vector.reciprocal(rsum[:, m, :], sums[:, m, :]).then_inc(inverted, 1)

        @block.vector
        def _(dve):
            def out(hn, half, stores):
                dve.wait_ge(pv_done, hn + 1)
                dve.wait_ge(rT_ready, hn + 1)
                dve.wait_ge(stored[half], stores)
                nc.vector.tensor_tensor(o_out[:, half, :], pv_bank, rT[:], ALU.mult).then_inc(o_ready, 1)

            def step(i, first):
                for u in range(UNITS):
                    n = UNITS * i + u
                    for a in range(2):
                        dve.wait_ge(scored[a], n + 1)
                        nc.vector.tensor_reduce(nmax[:, a, u % 2:u % 2 + 1], score_bank[a], axis=AX.XY, op=ALU.max,
                                                negate=True).then_inc(maxed[a], 1)
                        if a == 0:
                            invert(dve, i, u, first)
                    combine(dve, i, u, first)
                    if u == 3 and not first:
                        out(2 * i - 1, 1, 16 * (i - 1))
                    if u == 3 + UNITS // 2:
                        out(2 * i, 0, 16 * i)
            step(0, True)
            with dve.Fori(1, NGRP) as i:
                step(i, False)
            invert(dve, NGRP, 0, False)
            combine(dve, NGRP, 0, False)
            out(2 * NGRP - 1, 1, 16 * (NGRP - 1))

        def flip(pe, i, u, first):
            if first and u < 2:
                return
            m = (u - 2) % UNITS
            n = UNITS * i + u - 2
            pe.wait_ge(combined, n + 1)
            for c in range(SC):
                t = c // 4
                if c % 4 == 0 and not (first and u == 2):
                    pe.wait_ge(evacuated, 2 * (n - 1) + t + 1)
                last = nc.tensor.transpose(flip_bank[t][:, (c % 4) * P:(c % 4 + 1) * P],
                                           mix[:, m % 2, c * P:(c + 1) * P], ident[:])
                if c % 4 == 3:
                    last.then_inc(flipped, 1)

        def values(pe, i, half, nfirst):
            hn = 2 * i + half
            pe.wait_ge(evacuated, UNITS * (hn + 1))
            pe.wait_ge(v_in, 16 * i + 16)
            if not nfirst:
                pe.wait_ge(o_ready, hn)
            for c in range(SC):
                for h in range(G):
                    last = nc.tensor.matmul(pv_bank[h * DH:(h + 1) * DH, :], v_st[:, c, h * DH:(h + 1) * DH],
                                            mixT[:, half, c, h, :], start=c == 0, stop=c == SC - 1)
            last.then_inc(pv_done, 1)
            pe.wait_ge(rep_ready, hn + 1)
            if not nfirst:
                pe.wait_ge(rT_ready, hn)
            for q in range(HT):
                last = nc.tensor.transpose(r_bank[:, q * P:(q + 1) * P], rep[:, q].rearrange("p h d -> p (h d)"), ident[:])
            last.then_inc(rep_flipped, 1)

        @block.tensor
        def _(pe):
            def step(i, first):
                for u in range(UNITS):
                    half, h, qt = unit(u)
                    n = UNITS * i + u
                    if half == 0 and qt == 0:
                        pe.wait_ge(stack_in[h], 16 * 12 * i + 16 * 12)
                    for a in range(2):
                        if not (first and u == 0):
                            pe.wait_ge(exped[a], n)
                        for kb in range(S // 512):
                            last = nc.tensor.matmul(score_bank[a][:, kb, :],
                                                    q_st[:, h, a, half * HALF + qt * P:half * HALF + (qt + 1) * P],
                                                    k_st[:, h, a, kb * 512:(kb + 1) * 512], start=True, stop=True)
                        last.then_inc(scored[a], 1)
                    flip(pe, i, u, first)
                    if u == 2 and not first:
                        values(pe, i - 1, 1, False)
                    if u == 2 + UNITS // 2:
                        values(pe, i, 0, first)
            step(0, True)
            with pe.Fori(1, NGRP) as i:
                step(i, False)
            for u in range(2):
                flip(pe, NGRP, u, False)
            values(pe, NGRP - 1, 1, False)


def feed_forward(nc, ctx, x, oT, woT, w13, w2, facs, ident, out, psum):
    sb, sem = scopes(nc, ctx)
    TT = QB // P
    NBLK = T // QB
    wo_raw = sb("f_wo_raw", [P, KC, D], F32)
    wo_hi = sb("f_wo_hi", [P, KC, D], F32R)
    wo_lo = sb("f_wo_lo", [P, KC, D], F32R)
    o_raw = sb("f_o_raw", [P, KC, QB], F32)
    o_hi = sb("f_o_hi", [P, KC, QB], F32R)
    o_lo = sb("f_o_lo", [P, KC, QB], F32R)
    res = sb("f_res", [P, TT, D], F32)
    y = sb("f_y", [P, TT, D], F32)
    z = sb("f_z", [P, TT, D], F32)
    stats = sb("f_stats", [P, TT, 6], F32)
    pause = sb("f_pause", [P, 1], F32)
    mv = sb("f_mv", [P, 2, TT, 2], F32)
    rstd = sb("f_rstd", [P, 2, TT], F32)
    consts = sb("f_consts", [P, 1], F32)
    y_hi = sb("f_y_hi", [P, KC, QB], F16)
    y_lo = sb("f_y_lo", [P, KC, QB], F16)
    th = sb("f_th", [P, 2, QB], F32)
    gated = sb("f_gated", [P, 2, QB], F32)
    g_hi = sb("f_g_hi", [P, FC, QB], F16)
    g_lo = sb("f_g_lo", [P, FC, QB], F16)
    (w_in, x_in, w_hi_ok, w_lo_ok, o_hi_ok, o_lo_ok, projected, stat, powed, normed, dve_step, flipped, y_hi_ok, y_lo_ok,
     hidden, tanhed, gate_ok, g_hi_ok, g_lo_ok, down, stored, const_ok, hidden_used) = (sem("f_" + n) for n in (
         "w_in", "x_in", "w_hi_ok", "w_lo_ok", "o_hi_ok", "o_lo_ok", "projected", "stat", "powed", "normed", "dve_step",
         "flipped", "y_hi_ok", "y_lo_ok", "hidden", "tanhed", "gate_ok", "g_hi_ok", "g_lo_ok", "down", "stored", "const_ok", "hidden_used"))

    with nc.Block() as block:
        @block.sync
        def _(sp):
            sp.dma_start(wo_raw[:], woT.rearrange("(c p) d -> p c d", p=P)).then_inc(w_in, 16)
            with sp.Fori(0, NBLK) as k:
                sp.wait_ge(stat, 2 * TT * k)
                sp.dma_start(o_raw[:], oT[:, bass.ds(k * QB, QB)].rearrange("(c p) t -> p c t", p=P)).then_inc(x_in, 16)
                sp.dma_start(res[:], x[bass.ds(k * QB, QB), :].rearrange("(c p) d -> p c d", p=P)).then_inc(x_in, 16)
                for tt in range(TT):
                    sp.wait_ge(normed, 2 * TT * k + TT + tt + 1)
                    sp.dma_start(out[bass.ds(k * QB + tt * P, P), :], z[:, tt, :]).then_inc(stored, 16)
            sp.wait_ge(stored, 16 * TT * NBLK)

        @block.gpsimd
        def _(pool):
            nc.gpsimd.memset(consts[:], -0.5).then_inc(const_ok, 1)
            pool.wait_ge(const_ok, 1)
            with pool.Fori(0, NBLK) as k:
                for ln in range(2):
                    for tt in range(TT):
                        pool.wait_ge(stat, 2 * TT * k + TT * ln + tt + 1)
                        nc.gpsimd.tensor_tensor(rstd[:, ln, tt:tt + 1], mv[:, ln, tt, 1:2], consts[:], ALU.pow).then_inc(powed, 1)
                    if ln == 0:
                        for f in range(FC):
                            pool.wait_ge(g_hi_ok, FC * k + f + 1)
                            nc.gpsimd.tensor_tensor(g_lo[:, f, :], gated[:, f % 2, :], g_hi[:, f, :], ALU.subtract).then_inc(g_lo_ok, 1)

        def gate_copy(act, k, f):
            act.wait_ge(gate_ok, FC * k + f + 1)
            act.wait_ge(down, TT * k)
            nc.scalar.activation(g_hi[:, f, :], gated[:, f % 2, :], ACT.Copy).then_inc(g_hi_ok, 1)

        @block.scalar
        def _(act):
            act.wait_ge(w_in, 16)
            nc.scalar.activation(wo_hi[:].rearrange("p c d -> p (c d)"), wo_raw[:].rearrange("p c d -> p (c d)"), ACT.Copy).then_inc(w_hi_ok, 1)
            with act.Fori(0, NBLK) as k:
                act.wait_ge(x_in, 32 * k + 32)
                act.wait_ge(projected, TT * k)
                nc.scalar.activation(o_hi[:].rearrange("p c d -> p (c d)"), o_raw[:].rearrange("p c d -> p (c d)"), ACT.Copy).then_inc(o_hi_ok, 1)
                for c in range(KC):
                    act.wait_ge(flipped, KC * k + c + 1)
                    act.wait_ge(hidden, 2 * FC * k)
                    nc.scalar.activation(y_hi[:, c, :], psum[:, c % 2, :], ACT.Copy, scale=XSCALE).then_inc(y_hi_ok, 1)
                for f in range(FC):
                    act.wait_ge(hidden, 2 * FC * k + 2 * f + 1)
                    act.wait_ge(gate_ok, FC * k + f - 1) if f >= 2 else act.wait_ge(gate_ok, FC * k)
                    nc.scalar.activation(th[:, f % 2, :], psum[:, 2 + 2 * (f % 2), :], ACT.Tanh, scale=facs[:, 0:1]).then_inc(tanhed, 1)
                    if f >= 1:
                        gate_copy(act, k, f - 1)
                gate_copy(act, k, FC - 1)

        @block.vector
        def _(dve):
            dve.wait_ge(w_hi_ok, 1)
            nc.vector.tensor_tensor(wo_lo[:], wo_raw[:], wo_hi[:].bitcast(F32), ALU.subtract).then_inc(w_lo_ok, 1)

            def moments(ln, tt, base, count):
                dve.wait_ge(dve_step, base + 1)
                nc.vector.bn_stats(stats[:, tt, :], z[:, tt, :]).then_inc(dve_step, 1)
                dve.wait_ge(dve_step, base + 2)
                nc.vector.memset(pause[:], 0.0)
                nc.vector.bn_aggr(mv[:, ln, tt, :], stats[:, tt, :]).then_inc(dve_step, 1)
                dve.wait_ge(dve_step, base + 3)
                nc.vector.tensor_scalar(mv[:, ln, tt, 1:2], mv[:, ln, tt, 1:2], EPS, None, ALU.add).then_inc(stat, 1)

            def normalise(ln, tt, dst, count):
                dve.wait_ge(powed, count)
                nc.vector.tensor_scalar(dst, z[:, tt, :], mv[:, ln, tt, 0:1], rstd[:, ln, tt:tt + 1], ALU.subtract,
                                        ALU.mult).then_inc(normed, 1)
            with dve.Fori(0, NBLK) as k:
                dve.wait_ge(o_hi_ok, k + 1)
                dve.wait_ge(projected, TT * k)
                nc.vector.tensor_tensor(o_lo[:], o_raw[:], o_hi[:].bitcast(F32), ALU.subtract).then_inc(o_lo_ok, 1)
                for tt in range(TT):
                    dve.wait_ge(projected, TT * k + tt + 1)
                    dve.wait_ge(stored, 16 * TT * k)
                    nc.vector.tensor_tensor(z[:, tt, :], psum[:, 6 + tt % 2, :], res[:, tt, :], ALU.add).then_inc(dve_step, 1)
                    moments(0, tt, 6 * TT * k + 3 * tt, 0)
                    if tt:
                        normalise(0, tt - 1, y[:, tt - 1, :], 2 * TT * k + tt)
                normalise(0, TT - 1, y[:, TT - 1, :], 2 * TT * k + TT)
                for c in range(KC):
                    dve.wait_ge(y_hi_ok, KC * k + c + 1)
                    nc.vector.scalar_tensor_tensor(y_lo[:, c, :], psum[:, c % 2, :], XSCALE, y_hi[:, c, :], ALU.mult,
                                                   ALU.subtract).then_inc(y_lo_ok, 1)
                for f in range(FC):
                    dve.wait_ge(tanhed, FC * k + f + 1)
                    if f >= 2:
                        dve.wait_ge(g_lo_ok, FC * k + f - 1)
                    else:
                        dve.wait_ge(g_lo_ok, FC * k)
                    nc.vector.scalar_tensor_tensor(gated[:, f % 2, :], th[:, f % 2, :], 1.0, psum[:, 2 + 2 * (f % 2), :],
                                                   ALU.add, ALU.mult).then_inc(hidden_used, 1)
                    dve.wait_ge(hidden, 2 * FC * k + 2 * f + 2)
                    dve.wait_ge(hidden_used, FC * k + f + 1)
                    nc.vector.scalar_tensor_tensor(gated[:, f % 2, :], gated[:, f % 2, :], GSCALE, psum[:, 3 + 2 * (f % 2), :],
                                                   ALU.mult, ALU.mult).then_inc(gate_ok, 1)
                for tt in range(TT):
                    dve.wait_ge(down, TT * k + tt + 1)
                    nc.vector.scalar_tensor_tensor(z[:, tt, :], psum[:, 6 + tt % 2, :], facs[:, 1:2], y[:, tt, :], ALU.mult,
                                                   ALU.add).then_inc(dve_step, 1)
                    moments(1, tt, 6 * TT * k + 3 * (TT + tt), 0)
                    if tt:
                        normalise(1, tt - 1, z[:, tt - 1, :], 2 * TT * k + TT + tt)
                normalise(1, TT - 1, z[:, TT - 1, :], 2 * TT * k + 2 * TT)

        @block.tensor
        def _(pe):
            pe.wait_ge(w_lo_ok, 1)
            with pe.Fori(0, NBLK) as k:
                pe.wait_ge(o_lo_ok, k + 1)
                for tt in range(TT):
                    if tt >= 2:
                        pe.wait_ge(dve_step, 6 * TT * k + 3 * (tt - 2) + 1)
                    else:
                        pe.wait_ge(dve_step, 6 * TT * k)
                    n = 0
                    for op, wp in ((o_hi, wo_hi), (o_hi, wo_lo), (o_lo, wo_hi)):
                        for c in range(KC):
                            last = nc.tensor.matmul(psum[:, 6 + tt % 2, :], op[:, c, tt * P:(tt + 1) * P], wp[:, c, :],
                                                    start=n == 0, stop=n == 3 * KC - 1)
                            n += 1
                    last.then_inc(projected, 1)
                pe.wait_ge(normed, 2 * TT * k + TT)
                for c in range(KC):
                    pe.wait_ge(y_lo_ok, KC * k + c - 1) if c >= 2 else pe.wait_ge(y_lo_ok, KC * k)
                    for tt in range(TT):
                        last = nc.tensor.transpose(psum[:, c % 2, tt * P:(tt + 1) * P], y[:, tt, c * P:(c + 1) * P], ident[:])
                    last.then_inc(flipped, 1)
                pe.wait_ge(y_lo_ok, KC * k + KC)
                for f in range(FC):
                    pe.wait_ge(gate_ok, FC * k + f - 1) if f >= 2 else pe.wait_ge(gate_ok, FC * k)
                    for m in range(2):
                        n = 0
                        for part in (y_hi, y_lo):
                            for c in range(KC):
                                last = nc.tensor.matmul(psum[:, 2 + m + 2 * (f % 2), :], w13[:, m, c, f * P:(f + 1) * P],
                                                        part[:, c, :], start=n == 0, stop=n == 2 * KC - 1)
                                n += 1
                        last.then_inc(hidden, 1)
                pe.wait_ge(g_lo_ok, FC * k + FC)
                for tt in range(TT):
                    if tt >= 2:
                        pe.wait_ge(dve_step, 6 * TT * k + 3 * (TT + tt - 2) + 1)
                    n = 0
                    for part in (g_hi, g_lo):
                        for f in range(FC):
                            last = nc.tensor.matmul(psum[:, 6 + tt % 2, :], part[:, f, tt * P:(tt + 1) * P], w2[:, f, :],
                                                    start=n == 0, stop=n == 2 * FC - 1)
                            n += 1
                    last.then_inc(down, 1)


def build(nc, x, xT, wT, woT, lam, w1T, w3T, w2T, out):
    qk = nc.dram_tensor("qk_parts", [B, MATS, 2, D, S], F32, kind="Internal").ap()
    vs = nc.dram_tensor("v_rows", [B, S, D], F32, kind="Internal").ap()
    oT = nc.dram_tensor("o_T", [D, T], F32, kind="Internal").ap()
    with ExitStack() as whole:
        sb, sem = scopes(nc, whole)
        psum = whole.enter_context(nc.psum_tensor("psum", [P, 8, 512], F32))
        w13 = sb("w13", [P, 2, KC, HP], F16)
        w2 = sb("w2", [P, FC, D], F16)
        facs = sb("facs", [P, 2], F32)
        ident = sb("ident", [P, P], F32)
        id_ok = sem("id_ok")
        with nc.Block() as block:
            @block.gpsimd
            def _(pool):
                nc.gpsimd.memset(ident[:], 0.0).then_inc(id_ok, 1)
                pool.wait_ge(id_ok, 1)
                nc.gpsimd.affine_select(out=ident[:], in_=ident[:], compare_op=ALU.not_equal, fill=1.0, base=0,
                                        pattern=[[-1, P]], channel_multiplier=1).then_inc(id_ok, 1)
        with ExitStack() as ctx:
            ternary_weights(nc, ctx, w1T, w3T, w2T, w13, w2, facs)
        with ExitStack() as ctx:
            projections(nc, ctx, xT, wT, qk, vs, psum)
        with ExitStack() as ctx:
            attention(nc, ctx, lam, qk, vs, oT, ident, psum)
        with ExitStack() as ctx:
            feed_forward(nc, ctx, x, oT, woT, w13, w2, facs, ident, out, psum)


def kernel(**inputs):
    import numpy as np
    import concourse.bacc as bacc
    from concourse.bass_utils import run_bass_kernel_spmd as run

    a = {k.replace("L0_", ""): np.asarray(v) for k, v in inputs.items()}
    laid = {
        "x": a["attn_x"].reshape(T, D),
        "xT": a["attn_x"].transpose(0, 2, 1),
        "wT": np.stack([a[f"attn_{n}_w"].T for n in ("q1", "k1", "q2", "k2", "v")]),
        "woT": a["attn_o_w"].T,
        "lam": a["attn_lambda_param"],
        "w1T": a["ffn_w1"].T,
        "w3T": a["ffn_w3"].T,
        "w2T": a["ffn_w2"].T,
    }
    laid = {k: np.ascontiguousarray(v) for k, v in laid.items()}
    nc = bacc.Bacc("TRN2", target_bir_lowering=False, num_devices=1)
    args = [nc.dram_tensor(f"in_{k}", v.shape, mybir.dt.from_np(v.dtype), kind="ExternalInput").ap() for k, v in laid.items()]
    out = nc.dram_tensor("out", (T, D), F32, kind="ExternalOutput").ap()
    build(nc, *args, out)
    r = run(nc, [{f"in_{k}": v for k, v in laid.items()}], core_ids=[0])
    return r.results[0]["out"].reshape(B, S, D)
```

```python
from contextlib import ExitStack

import concourse.bass as bass
from concourse import mybir

F32 = mybir.dt.float32
F32R = mybir.dt.float32r
F16 = mybir.dt.float16
ALU = mybir.AluOpType
ACT = mybir.ActivationFunctionType
AX = mybir.AxisListType

P = 128
B, S, D = 2, 1024, 512
H, DH = 16, 32
HIDDEN = int(2 * D * 4 / 3)
T = B * S
KC = D // P
FC = -(-HIDDEN // P)
HP = FC * P
LAST = HIDDEN - (FC - 1) * P
G = P // DH
NG = H // G
QB = 512
NQB = S // QB
SC = S // P
QT = QB // P
UNITS = QT * G
NSTEP = B * NQB * NG
NBLK = B * NQB
MATS = 4
NW = MATS + 1
EPS = 1e-5
SCORE_SCALE = float(DH) ** -0.5
XSCALE = 1024.0
GSCALE = 2.0 ** -24


def scopes(nc, ctx, sems=None):
    def sb(name, shape, dt):
        return ctx.enter_context(nc.sbuf_tensor(name, shape, dt))

    def sem(name):
        return (sems or ctx).enter_context(nc.semaphore(name))
    return sb, sem


SIDE = 6
PV_SLOT = {"project": {2: 3, 6: 0, 10: 1, 14: 2}, "feed": {3: 3, 6: 0, 10: 1, 14: 2}}
JOB_SLOT = {u: k for k, u in enumerate((3, 4, 5, 7, 8, 9, 11, 12, 13, 15))}
NJOB = len(JOB_SLOT)
JOBS = [("qk", m, tb) for m in range(MATS) for tb in range(S // 512)] + [("v", MATS, tb) for tb in range(S // 512)]
GATES = -(-FC // 2)
GATE_SLOT = {u: k for k, u in enumerate((7, 8, 9, 11, 12, 13))}
F0 = NG
NTILE = NSTEP - F0


class Projections:

    def __init__(self, nc, ctx, sems, xT, w5, qk, vs, psum):
        self.nc, self.xT, self.w5, self.qk, self.vs, self.psum = nc, xT, w5, qk, vs, psum
        sb, sem = scopes(nc, ctx, sems)
        self.w_raw = sb("p_w_raw", [P, NW, KC, P], F32)
        self.w_hi = sb("p_w_hi", [P, NW, KC, P], F32R)
        self.w_lo = sb("p_w_lo", [P, NW, KC, P], F32R)
        self.x_raw = sb("p_x_raw", [P, KC, S], F32)
        self.x_hi = sb("p_x_hi", [P, KC, S], F32R)
        self.x_lo = sb("p_x_lo", [P, KC, S], F32R)
        self.out_hi = sb("p_out_hi", [P, 2, 512], F32R)
        self.out_lo = sb("p_out_lo", [P, 2, 512], F32R)
        self.out_v = sb("p_out_v", [P, 2, 512], F32)
        self.size = 4 * (3 * NW * KC * P + 3 * KC * S + 3 * 2 * 512)
        self.w_in, self.x_in, self.w_hi_ok, self.w_lo_ok, self.x_hi_ok, self.x_lo_dve, self.x_lo_pool = (
            sem("p_" + n) for n in ("w_in", "x_in", "w_hi_ok", "w_lo_ok", "x_hi_ok", "x_lo_dve", "x_lo_pool"))
        self.product, self.got_hi, self.got_lo = (sem("p_" + n) for n in ("product", "got_hi", "got_lo"))
        self.stored = [sem(f"p_stored{i}") for i in range(2)]

    def load_x(self, sp, b):
        if b:
            sp.wait_ge(self.x_lo_dve, 2 * b)
            sp.wait_ge(self.x_lo_pool, 2 * b)
        sp.dma_start(self.x_raw[:], self.xT[b].rearrange("(c p) t -> p c t", p=P)).then_inc(self.x_in, 16)

    def load_w(self, sp, j, first):
        if not first:
            sp.wait_ge(self.w_lo_ok, NW * j)
        sp.dma_start(self.w_raw[:].rearrange("p m c f -> p (m c f)"),
                     self.w5[bass.ds(j % NG, 1)].rearrange("a p n -> p (a n)")).then_inc(self.w_in, 16)

    def split_x_hi(self, act, b, c):
        act.wait_ge(self.x_in, 16 * (b + 1))
        if b:
            act.wait_ge(self.product, NJOB * NG * b)
        self.nc.scalar.activation(self.x_hi[:, c, :], self.x_raw[:, c, :], ACT.Copy).then_inc(self.x_hi_ok, 1)

    def split_x_lo(self, eng, vector, b, c, done):
        eng.wait_ge(self.x_hi_ok, KC * b + c + 1)
        vector.tensor_tensor(self.x_lo[:, c, :], self.x_raw[:, c, :], self.x_hi[:, c, :].bitcast(F32),
                             ALU.subtract).then_inc(done, 1)

    def split_w_hi(self, act, j, first):
        act.wait_ge(self.w_in, 16 * j + 16)
        if not first:
            act.wait_ge(self.product, NJOB * j)
        self.nc.scalar.activation(self.w_hi[:].rearrange("p m c f -> p (m c f)"),
                                  self.w_raw[:].rearrange("p m c f -> p (m c f)"), ACT.Copy).then_inc(self.w_hi_ok, 1)

    def split_w_lo(self, pool, j, m):
        pool.wait_ge(self.w_hi_ok, j + 1)
        self.nc.gpsimd.tensor_tensor(self.w_lo[:, m].rearrange("p c f -> p (c f)"),
                                     self.w_raw[:, m].rearrange("p c f -> p (c f)"),
                                     self.w_hi[:, m].rearrange("p c f -> p (c f)").bitcast(F32),
                                     ALU.subtract).then_inc(self.w_lo_ok, 1)

    def multiply(self, pe, j, k, bank, halves=(0, 1)):
        kind, m, tb = JOBS[k]
        nc, ps = self.nc, self.psum[:, bank, :]
        if 0 in halves:
            pe.wait_ge(self.w_lo_ok, NW * j + m + 1)
        terms = ((self.x_hi, self.w_hi), (self.x_hi, self.w_lo), (self.x_lo, self.w_hi))
        if kind == "qk":
            groups = [(ps, lambda xp, wp, c: (wp[:, m, c, :], xp[:, c, tb * 512:(tb + 1) * 512]))]
        else:
            groups = [(ps[:, q * P:(q + 1) * P],
                       lambda xp, wp, c, q=q: (xp[:, c, tb * 512 + q * P:tb * 512 + (q + 1) * P], wp[:, m, c, :]))
                      for q in range(4)]
        products = [(dst, operands(xp, wp, c), n * KC + c) for dst, operands in groups
                    for n, (xp, wp) in enumerate(terms) for c in range(KC)]
        for half in halves:
            for dst, (stationary, moving), n in products[half * len(products) // 2:(half + 1) * len(products) // 2]:
                last = nc.tensor.matmul(dst, stationary, moving, start=n == 0, stop=n == 3 * KC - 1)
        if 1 in halves:
            last.then_inc(self.product, 1)

    def take_hi(self, act, j, k, bank, first):
        kind, m, tb = JOBS[k]
        act.wait_ge(self.product, NJOB * j + k + 1)
        if not (first and k < 2):
            act.wait_ge(self.stored[k % 2], (NJOB // 2) * 32 * j + k // 2 * 32)
        if kind == "v":
            self.nc.scalar.activation(self.out_v[:, k % 2, 0:256], self.psum[:, bank, 0:256], ACT.Copy).then_inc(self.got_hi, 1)
        else:
            self.nc.scalar.activation(self.out_hi[:, k % 2, :], self.psum[:, bank, :], ACT.Copy,
                                      scale=SCORE_SCALE if m % 2 == 0 else 1.0).then_inc(self.got_hi, 1)

    def take_lo(self, dve, j, k, bank):
        kind, m, tb = JOBS[k]
        dve.wait_ge(self.got_hi, NJOB * j + k + 1)
        if kind == "v":
            self.nc.vector.tensor_copy(self.out_v[:, k % 2, 256:512], self.psum[:, bank, 256:512]).then_inc(self.got_lo, 1)
        else:
            self.nc.vector.scalar_tensor_tensor(self.out_lo[:, k % 2, :], self.psum[:, bank, :],
                                                SCORE_SCALE if m % 2 == 0 else 1.0,
                                                self.out_hi[:, k % 2, :].bitcast(F32), ALU.mult, ALU.subtract).then_inc(self.got_lo, 1)

    def store(self, sp, j, b, k):
        kind, m, tb = JOBS[k]
        f = (j - NG * b) * P
        f = f if isinstance(f, int) else sp.snap(f)
        sp.wait_ge(self.got_lo, NJOB * j + k + 1)
        if kind == "qk":
            for part, stage in ((1, self.out_lo), (0, self.out_hi)):
                sp.dma_start(self.qk[b, m, part, bass.ds(f, P), tb * 512:(tb + 1) * 512],
                             stage[:, k % 2, :].bitcast(F32)).then_inc(self.stored[k % 2], 16)
        else:
            for c in (1, 0):
                sp.dma_start(self.vs[b, tb * 512 + c * 256:tb * 512 + (c + 1) * 256, bass.ds(f, P)].rearrange("(q p) f -> p q f", p=P),
                             self.out_v[:, k % 2, c * 256:(c + 1) * 256].rearrange("p (q f) -> p q f", q=2)).then_inc(self.stored[k % 2], 16)


class FeedForward:

    def __init__(self, nc, ctx, sems, x, oT, wq, wod, facs, ident, out, psum):
        self.nc, self.x, self.oT, self.wq, self.wod = nc, x, oT, wq, wod
        self.facs, self.ident, self.out, self.psum = facs, ident, out, psum
        sb, sem = scopes(nc, ctx, sems)
        self.w13 = sb("f_w13", [P, 2, KC, HP], F16)
        self.w2 = sb("f_w2", [P, FC, D], F16)
        self.wo_hi = sb("f_wo_hi", [P, KC, D], F32R)
        self.wo_lo = sb("f_wo_lo", [P, KC, D], F32R)
        self.o_raw = sb("f_o_raw", [P, KC, P], F32)
        self.o_hi = sb("f_o_hi", [P, KC, P], F32R)
        self.o_lo = sb("f_o_lo", [P, KC, P], F32R)
        self.res = sb("f_res", [P, D], F32)
        self.z = sb("f_z", [P, 2, D], F32)
        self.y = sb("f_y", [P, D], F32)
        self.fin = sb("f_fin", [P, D], F32)
        self.stats = sb("f_stats", [P, 2, 6], F32)
        self.mv = sb("f_mv", [P, 2, 2], F32)
        self.rstd = sb("f_rstd", [P, 2], F32)
        self.pause = sb("f_pause", [P, 1], F32)
        self.expo = sb("f_expo", [P, 1], F32)
        self.y_hi = sb("f_y_hi", [P, KC, P], F16)
        self.y_lo = sb("f_y_lo", [P, KC, P], F16)
        self.th = sb("f_th", [P, 2, 256], F32)
        self.half_gate = sb("f_half_gate", [P, 256], F32)
        self.gated = sb("f_gated", [P, 2, 256], F32)
        self.g_hi = sb("f_g_hi", [P, FC, P], F16)
        self.g_lo = sb("f_g_lo", [P, FC, P], F16)
        self.size = (2 * (2 * KC * HP + FC * D + 2 * KC * P + 2 * FC * P)
                     + 4 * (2 * KC * D + 3 * KC * P + 5 * D + 2 * 6 + 2 * 2 + 2 + 2 + 5 * 256))
        self.wo_in = sem("f_wo_in")
        self.w13_in = sem("f_w13_in")
        self.w2_in = sem("f_w2_in")
        self.expo_ok = sem("f_expo_ok")
        self.x_in = sem("f_x_in")
        self.o_hi_ok = sem("f_o_hi_ok")
        self.o_lo_ok = sem("f_o_lo_ok")
        self.projected = sem("f_projected")
        self.stat1 = sem("f_stat1")
        self.stat2 = sem("f_stat2")
        self.step1 = sem("f_step1")
        self.step2 = sem("f_step2")
        self.pow1 = sem("f_pow1")
        self.pow2 = sem("f_pow2")
        self.y_ok = sem("f_y_ok")
        self.fin_ok = sem("f_fin_ok")
        self.flipped = sem("f_flipped")
        self.y_hi_ok = sem("f_y_hi_ok")
        self.y_lo_ok = sem("f_y_lo_ok")
        self.hidden = sem("f_hidden")
        self.tanhed = sem("f_tanhed")
        self.halved = sem("f_halved")
        self.gate_ok = sem("f_gate_ok")
        self.g_hi_ok = sem("f_g_hi_ok")
        self.g_lo_ok = sem("f_g_lo_ok")
        self.down = sem("f_down")
        self.stored = sem("f_stored")

    def load_weights(self, sp):
        for dst, src, done in ((self.wo_hi[:].rearrange("p c d -> p (c d)").bitcast(F32), self.wod[0], self.wo_in),
                               (self.wo_lo[:].rearrange("p c d -> p (c d)").bitcast(F32), self.wod[1], self.wo_in),
                               (self.w13[:, 0].rearrange("p c f -> p (c f)"), self.wq[2], self.w13_in),
                               (self.w13[:, 1].rearrange("p c f -> p (c f)"), self.wq[1], self.w13_in),
                               (self.w2[:].rearrange("p c d -> p (c d)"), self.wq[0], self.w2_in)):
            sp.dma_start(dst, src).then_inc(done, 16)

    def load(self, sp, t):
        sp.dma_start(self.o_raw[:], self.oT[:, bass.ds(t * P, P)].rearrange("(c p) t -> p c t", p=P)).then_inc(self.x_in, 16)
        sp.dma_start(self.res[:], self.x[bass.ds(t * P, P), :]).then_inc(self.x_in, 16)

    def split_hi(self, act, t):
        act.wait_ge(self.x_in, 32 * t + 32)
        self.nc.scalar.activation(self.o_hi[:].rearrange("p c t -> p (c t)"), self.o_raw[:].rearrange("p c t -> p (c t)"),
                                  ACT.Copy).then_inc(self.o_hi_ok, 1)

    def split_lo(self, pool, t):
        pool.wait_ge(self.o_hi_ok, t + 1)
        self.nc.gpsimd.tensor_tensor(self.o_lo[:], self.o_raw[:], self.o_hi[:].bitcast(F32), ALU.subtract).then_inc(self.o_lo_ok, 1)

    def project(self, pe, t, bank, half):
        if half == 0:
            pe.wait_ge(self.o_lo_ok, t + 1)
        products = [(op, wp, c) for op, wp in ((self.o_hi, self.wo_hi), (self.o_hi, self.wo_lo), (self.o_lo, self.wo_hi))
                    for c in range(KC)]
        for n in range(half * 6, half * 6 + 6):
            op, wp, c = products[n]
            last = self.nc.tensor.matmul(self.psum[:, bank, :], op[:, c, :], wp[:, c, :], start=n == 0, stop=n == 3 * KC - 1)
        if half:
            last.then_inc(self.projected, 1)

    def moments(self, dve, t, ln, step, stat):
        dve.wait_ge(step, 3 * t + 1)
        self.nc.vector.bn_stats(self.stats[:, ln, :], self.z[:, ln, :]).then_inc(step, 1)
        dve.wait_ge(step, 3 * t + 2)
        self.nc.vector.memset(self.pause[:], 0.0)
        self.nc.vector.bn_aggr(self.mv[:, ln, :], self.stats[:, ln, :]).then_inc(step, 1)
        dve.wait_ge(step, 3 * t + 3)
        self.nc.vector.tensor_scalar(self.mv[:, ln, 1:2], self.mv[:, ln, 1:2], EPS, None, ALU.add).then_inc(stat, 1)

    def power(self, pool, t, ln, stat, done):
        pool.wait_ge(stat, t + 1)
        self.nc.gpsimd.tensor_tensor(self.rstd[:, ln:ln + 1], self.mv[:, ln, 1:2], self.expo[:], ALU.pow).then_inc(done, 1)

    def residual(self, dve, t, bank):
        dve.wait_ge(self.projected, t + 1)
        self.nc.vector.tensor_tensor(self.z[:, 0, :], self.psum[:, bank, :], self.res[:], ALU.add).then_inc(self.step1, 1)
        self.moments(dve, t, 0, self.step1, self.stat1)

    def norm1(self, dve, t):
        dve.wait_ge(self.pow1, t + 1)
        self.nc.vector.tensor_scalar(self.y[:], self.z[:, 0, :], self.mv[:, 0, 0:1], self.rstd[:, 0:1], ALU.subtract,
                                     ALU.mult).then_inc(self.y_ok, 1)

    def flip(self, pe, t, bank):
        pe.wait_ge(self.y_ok, t + 1)
        for c in range(KC):
            last = self.nc.tensor.transpose(self.psum[:, bank, c * P:(c + 1) * P], self.y[:, c * P:(c + 1) * P], self.ident[:])
        last.then_inc(self.flipped, 1)

    def y_parts_hi(self, act, t, bank):
        act.wait_ge(self.flipped, t + 1)
        self.nc.scalar.activation(self.y_hi[:].rearrange("p c t -> p (c t)"), self.psum[:, bank, :], ACT.Copy,
                                  scale=XSCALE).then_inc(self.y_hi_ok, 1)

    def y_parts_lo(self, dve, t, bank):
        dve.wait_ge(self.y_hi_ok, t + 1)
        self.nc.vector.scalar_tensor_tensor(self.y_lo[:].rearrange("p c t -> p (c t)"), self.psum[:, bank, :], XSCALE,
                                            self.y_hi[:].rearrange("p c t -> p (c t)"), ALU.mult, ALU.subtract).then_inc(self.y_lo_ok, 1)

    def gate_width(self, q):
        return min(2, FC - 2 * q) * P

    def hidden_pair(self, pe, t, q, bank, m):
        if q == 0 and m == 0:
            pe.wait_ge(self.y_lo_ok, t + 1)
        for f in range(self.gate_width(q) // P):
            n = 0
            for part in (self.y_hi, self.y_lo):
                for c in range(KC):
                    last = self.nc.tensor.matmul(self.psum[:, bank, m * 256 + f * P:m * 256 + (f + 1) * P],
                                                 self.w13[:, m, c, (2 * q + f) * P:(2 * q + f + 1) * P], part[:, c, :],
                                                 start=n == 0, stop=n == 2 * KC - 1)
                    n += 1
        if m:
            last.then_inc(self.hidden, 1)

    def tanh(self, act, t, q, bank):
        w = self.gate_width(q)
        act.wait_ge(self.hidden, GATES * t + q + 1)
        if q >= 2:
            act.wait_ge(self.halved, GATES * t + q - 1)
        self.nc.scalar.activation(self.th[:, q % 2, 0:w], self.psum[:, bank, 0:w], ACT.Tanh, scale=self.facs[:, 0:1]).then_inc(self.tanhed, 1)

    def gate(self, dve, t, q, bank):
        w = self.gate_width(q)
        dve.wait_ge(self.tanhed, GATES * t + q + 1)
        self.nc.vector.scalar_tensor_tensor(self.half_gate[:, 0:w], self.th[:, q % 2, 0:w], 1.0, self.psum[:, bank, 0:w],
                                            ALU.add, ALU.mult).then_inc(self.halved, 1)
        if q >= 2:
            dve.wait_ge(self.g_lo_ok, GATES * t + q - 1)
        dve.wait_ge(self.halved, GATES * t + q + 1)
        self.nc.vector.scalar_tensor_tensor(self.gated[:, q % 2, 0:w], self.half_gate[:, 0:w], GSCALE,
                                            self.psum[:, bank, 256:256 + w], ALU.mult, ALU.mult).then_inc(self.gate_ok, 1)

    def gate_hi(self, act, t, q):
        w = self.gate_width(q)
        act.wait_ge(self.gate_ok, GATES * t + q + 1)
        self.nc.scalar.activation(self.g_hi[:, 2 * q:2 * q + w // P, :].rearrange("p c t -> p (c t)"), self.gated[:, q % 2, 0:w],
                                  ACT.Copy).then_inc(self.g_hi_ok, 1)

    def gate_lo(self, pool, t, q):
        w = self.gate_width(q)
        pool.wait_ge(self.g_hi_ok, GATES * t + q + 1)
        self.nc.gpsimd.tensor_tensor(self.g_lo[:, 2 * q:2 * q + w // P, :].rearrange("p c t -> p (c t)"), self.gated[:, q % 2, 0:w],
                                     self.g_hi[:, 2 * q:2 * q + w // P, :].rearrange("p c t -> p (c t)"), ALU.subtract).then_inc(self.g_lo_ok, 1)

    def back(self, pe, t, bank, piece):
        chunks = range(3 * piece, min(FC, 3 * piece + 3))
        pe.wait_ge(self.g_lo_ok, GATES * t + chunks[-1] // 2 + 1)
        for f in chunks:
            for part in (self.g_hi, self.g_lo):
                last = self.nc.tensor.matmul(self.psum[:, bank, :], part[:, f, :], self.w2[:, f, :],
                                             start=f == 0 and part is self.g_hi, stop=f == FC - 1 and part is self.g_lo)
        if piece == 3:
            last.then_inc(self.down, 1)

    def residual2(self, dve, t, bank):
        dve.wait_ge(self.down, t + 1)
        self.nc.vector.scalar_tensor_tensor(self.z[:, 1, :], self.psum[:, bank, :], self.facs[:, 1:2], self.y[:], ALU.mult,
                                            ALU.add).then_inc(self.step2, 1)
        self.moments(dve, t, 1, self.step2, self.stat2)

    def norm2(self, dve, t):
        dve.wait_ge(self.pow2, t + 1)
        self.nc.vector.tensor_scalar(self.fin[:], self.z[:, 1, :], self.mv[:, 1, 0:1], self.rstd[:, 1:2], ALU.subtract,
                                     ALU.mult).then_inc(self.fin_ok, 1)

    def store(self, sp, t):
        sp.wait_ge(self.fin_ok, t + 1)
        sp.dma_start(self.out[bass.ds(t * P, P), :], self.fin[:]).then_inc(self.stored, 16)

def prepare(nc, ctx, proj, wff, woT, wq, wod, facs, ones):
    sb, sem = scopes(nc, ctx)
    N = KC * HP
    raw = sb("q_raw", [P, N], F32)
    below = sb("q_below", [P, N], F16)
    tern = sb("q_tern", [P, N], F16)
    part = sb("q_part", [P, 1], F32)
    half = sb("q_half", [P, 2], F32)
    wo_raw = sb("q_wo_raw", [P, KC * D], F32)
    wo_hi = sb("q_wo_hi", [P, KC * D], F32R)
    wo_lo = sb("q_wo_lo", [P, KC * D], F32R)
    raw_in, summed, reduced, halved, compared, ternary, stored, wo_in, wo_hi_ok, wo_lo_ok, wo_stored, ones_ok, facs_ok = (
        sem("q_" + n) for n in ("raw_in", "summed", "reduced", "halved", "compared", "ternary", "stored", "wo_in",
                                "wo_hi_ok", "wo_lo_ok", "wo_stored", "ones_ok", "facs_ok"))
    BANKS = 5
    sum_bank = proj.psum[:, 7, 0:1]

    with nc.Block() as block:
        @block.sync
        def _(sp):
            proj.load_w(sp, 0, True)
            proj.load_x(sp, 0)
            sp.dma_start(wo_raw[:].rearrange("p (c d) -> p c d", c=KC), woT.rearrange("(c p) d -> p c d", p=P)).then_inc(wo_in, 16)
            sp.dma_start(raw[:], wff[0]).then_inc(raw_in, 16)

            def stores(j):
                for k in range(NJOB):
                    if k == 4:
                        proj.load_w(sp, j + 1, False)
                    proj.store(sp, j, 0, k)
            stores(0)
            sp.wait_ge(wo_lo_ok, 1)
            sp.dma_start(wod[0], wo_hi[:].bitcast(F32)).then_inc(wo_stored, 16)
            sp.dma_start(wod[1], wo_lo[:].bitcast(F32)).then_inc(wo_stored, 16)
            proj.load_x(sp, 1)
            with sp.Fori(1, NG) as j:
                stores(j)
                sp.wait_ge(ternary, j)
                sp.dma_start(wq[bass.ds(j - 1, 1)].rearrange("a p n -> p (a n)"), tern[:]).then_inc(stored, 16)
                sp.wait_ge(stored, 16 * j)
                sp.dma_start(raw[:], wff[bass.ds(j % (NG - 1), 1)].rearrange("a p n -> p (a n)")).then_inc(raw_in, 16)
            sp.wait_ge(wo_stored, 32)
            sp.wait_ge(stored, 16 * (NG - 1))
            sp.wait_ge(raw_in, 16 * NG)

        @block.gpsimd
        def _(pool):
            nc.gpsimd.memset(ones[:], 1.0).then_inc(ones_ok, 1)
            for c in (2, 3):
                proj.split_x_lo(pool, nc.gpsimd, 0, c, proj.x_lo_pool)
            for m in range(NW):
                proj.split_w_lo(pool, 0, m)
            with pool.Fori(1, NG) as j:
                for m in range(NW):
                    proj.split_w_lo(pool, j, m)

        @block.scalar
        def _(act):
            proj.split_w_hi(act, 0, True)
            for c in range(KC):
                proj.split_x_hi(act, 0, c)
            for k in range(NJOB):
                proj.take_hi(act, 0, k, k % BANKS, True)
            act.wait_ge(wo_in, 16)
            nc.scalar.activation(wo_hi[:], wo_raw[:], ACT.Copy).then_inc(wo_hi_ok, 1)
            with act.Fori(1, NG) as j:
                proj.split_w_hi(act, j, False)
                for k in range(NJOB):
                    proj.take_hi(act, j, k, k % BANKS, False)

        @block.vector
        def _(dve):
            nc.vector.memset(facs[:, 1:2], 4.0 / (XSCALE * XSCALE * GSCALE)).then_inc(facs_ok, 1)
            for c in (0, 1):
                proj.split_x_lo(dve, nc.vector, 0, c, proj.x_lo_dve)
            for k in range(NJOB):
                proj.take_lo(dve, 0, k, k % BANKS)
            dve.wait_ge(wo_hi_ok, 1)
            nc.vector.tensor_tensor(wo_lo[:], wo_raw[:], wo_hi[:].bitcast(F32), ALU.subtract).then_inc(wo_lo_ok, 1)
            with dve.Fori(1, NG) as j:
                for k in range(NJOB):
                    proj.take_lo(dve, j, k, k % BANKS)
                    if k == 2:
                        dve.wait_ge(raw_in, 16 * j)
                        nc.vector.tensor_reduce(part[:], raw[:], axis=AX.X, op=ALU.add,
                                                apply_absolute_value=True).then_inc(summed, 1)
                    if k == 6:
                        dve.wait_ge(reduced, j)
                        for n, sign in enumerate((0.5, -0.5)):
                            nc.vector.tensor_scalar(half[:, n:n + 1], sum_bank, sign / (HIDDEN * D), None, ALU.mult).then_inc(halved, 1)
                        dve.wait_ge(halved, 2 * j)
                        nc.vector.tensor_scalar(below[:], raw[:], half[:, 1:2], None, ALU.is_lt).then_inc(compared, 1)
                        nc.vector.tensor_scalar(facs[:, 0:1], half[:, 0:1], 1.0 / XSCALE, None, ALU.mult)
                        dve.wait_ge(facs_ok, j)
                        nc.vector.tensor_tensor(facs[:, 1:2], facs[:, 1:2], half[:, 0:1], ALU.mult).then_inc(facs_ok, 1)
                    if k == 7:
                        dve.wait_ge(compared, j)
                        nc.vector.scalar_tensor_tensor(tern[:], raw[:], half[:, 0:1], below[:], ALU.is_gt,
                                                       ALU.subtract).then_inc(ternary, 1)

        @block.tensor
        def _(pe):
            pe.wait_ge(proj.x_lo_dve, 2)
            pe.wait_ge(proj.x_lo_pool, 2)
            pe.wait_ge(ones_ok, 1)
            for k in range(NJOB):
                if k >= BANKS:
                    pe.wait_ge(proj.got_lo, k - BANKS + 1)
                proj.multiply(pe, 0, k, k % BANKS)
            with pe.Fori(1, NG) as j:
                for k in range(NJOB):
                    pe.wait_ge(proj.got_lo, NJOB * j + k - BANKS + 1)
                    proj.multiply(pe, j, k, k % BANKS)
                    if k == 5:
                        pe.wait_ge(summed, j)
                        nc.tensor.matmul(sum_bank, ones[:], part[:], start=True, stop=True).then_inc(reduced, 1)


def attention(nc, ctx, lam, qk, vs, oT, ones, ident, psum, proj, ffn):
    sb, sem = scopes(nc, ctx)
    k_st = sb("k_st", [3 * DH, G, 2, S], F32R)
    q_st = sb("q_st", [3 * DH, G, 2, QB], F32R)
    v_st = sb("v_st", [P, SC, P], F32)
    e = sb("e", [P, 2, 2, S], F32)
    mix = sb("mix", [P, 2, S], F32)
    mixT = sb("mixT", [P, 2, SC, G, P], F32)
    nmax = sb("nmax", [P, 2, 2], F32)
    sums = sb("sums", [P, UNITS, 2], F32)
    rsum = sb("rsum", [P, UNITS], F32)
    rsum2 = sb("rsum2", [P, UNITS], F32)
    coef = sb("coef", [P, UNITS], F32)
    nlam = sb("nlam", [P, NSTEP * G], F32)
    nlam4 = sb("nlam4", [P, G], F32)
    lam_raw = sb("lam_raw", [P, H], F32)
    rep = sb("rep", [P, G, DH], F32)
    rT = sb("rT", [P, P], F32)
    o_out = sb("o_out", [P, 2, P], F32)

    score_bank = [psum[:, 2 * a:2 * a + 2, :] for a in range(2)]
    flip_bank = [psum[:, 4 + i, :] for i in range(2)]
    pv_bank = psum[:, SIDE, 0:P]
    r_bank = psum[:, SIDE, P:2 * P]

    stack_in = [sem(f"a_stack_in{h}") for h in range(G)]
    scored = [sem(f"a_scored{a}") for a in range(2)]
    maxed = [sem(f"a_maxed{a}") for a in range(2)]
    exped = [sem(f"a_exped{a}") for a in range(2)]
    stored = [sem(f"a_stored{i}") for i in range(2)]
    (v_in, inverted, inverted2, weighted, combined, flipped, evacuated, pv_done, rep_ready, rep_flipped, rT_ready, o_ready,
     lam_in, lam_step) = (sem("a_" + n) for n in (
         "v_in", "inverted", "inverted2", "weighted", "combined", "flipped", "evacuated", "pv_done", "rep_ready",
         "rep_flipped", "rT_ready", "o_ready", "lam_in", "lam_step"))

    def is_first(i):
        return isinstance(i, int) and i == 0

    def load_stack(sp, i, h):
        b, tb, g = i // (NQB * NG), (i // NG) % NQB, i % NG
        for a in range(2):
            for slot, part in enumerate((0, 0, 1)):
                src = qk[bass.ds(b, 1), 2 * a, part, bass.ds(g * P + h * DH, DH), bass.ds(tb * QB, QB)]
                sp.dma_start(q_st[slot * DH:(slot + 1) * DH, h, a, :].bitcast(F32),
                             src.rearrange("a f t -> f (a t)")).then_inc(stack_in[h], 16)
            for slot, part in enumerate((0, 1, 0)):
                src = qk[bass.ds(b, 1), 2 * a + 1, part, bass.ds(g * P + h * DH, DH), :]
                sp.dma_start(k_st[slot * DH:(slot + 1) * DH, h, a, :].bitcast(F32),
                             src.rearrange("a f t -> f (a t)")).then_inc(stack_in[h], 16)

    def load_v(sp, i):
        if not is_first(i):
            sp.wait_ge(pv_done, QT * i)
        b, g = i // (NQB * NG), i % NG
        sp.dma_start(v_st[:], vs[bass.ds(b, 1), :, bass.ds(g * P, P)].rearrange("a (c p) f -> p (a c) f", p=P)).then_inc(v_in, 16)

    def store_o(sp, i, q):
        sp.wait_ge(o_ready, QT * i + q + 1)
        dst = oT[bass.ds((i % NG) * P, P), bass.ds((i // NG) * QB + q * P, P)]
        sp.dma_start(dst, o_out[:, q % 2, :]).then_inc(stored[q % 2], 16)

    def exponentials(act, i, u, a):
        n = UNITS * i + u
        act.wait_ge(maxed[a], n + 1)
        if not (is_first(i) and u < 2):
            act.wait_ge(combined, n - 1)
        nc.scalar.activation(e[:, a, u % 2, :], score_bank[a].rearrange("p b k -> p (b k)"), ACT.Exp,
                             bias=nmax[:, a, u % 2:u % 2 + 1], accum_out=sums[:, u, a:a + 1]).then_inc(exped[a], 1)

    def evacuate(act, i, u, t):
        if is_first(i) and u < 2:
            return
        m = (u - 2) % UNITS
        q, h = divmod(m, G)
        n = UNITS * i + u - 2
        if t == 0 and h == 0 and not (is_first(i) and m < 2 * G):
            act.wait_ge(pv_done, QT * i + q - 1)
        act.wait_ge(flipped, 2 * n + t + 1)
        nc.scalar.activation(mixT[:, q % 2, t * 4:t * 4 + 4, h, :],
                             flip_bank[t].rearrange("p (c q) -> p c q", q=P), ACT.Copy).then_inc(evacuated, 1)

    def take_r(act, qn, first):
        act.wait_ge(rep_flipped, qn + 1)
        if not first:
            act.wait_ge(o_ready, qn)
        nc.scalar.activation(rT[:], r_bank, ACT.Copy).then_inc(rT_ready, 1)

    def maximum(dve, i, u, a):
        dve.wait_ge(scored[a], UNITS * i + u + 1)
        nc.vector.tensor_reduce(nmax[:, a, u % 2:u % 2 + 1], score_bank[a], axis=AX.XY, op=ALU.max,
                                negate=True).then_inc(maxed[a], 1)

    def weigh(dve, i, u):
        if is_first(i) and u == 0:
            return
        m = (u - 1) % UNITS
        n = UNITS * i + u - 1
        if m == 0:
            dve.wait_ge(lam_step, i + 2)
        for a in range(2):
            dve.wait_ge(exped[a], n + 1)
        nc.vector.reciprocal(rsum2[:, m:m + 1], sums[:, m, 1:2]).then_inc(inverted2, 1)
        dve.wait_ge(inverted2, n + 1)
        nc.vector.scalar_tensor_tensor(coef[:, m:m + 1], sums[:, m, 0:1], nlam4[:, m % G:m % G + 1], rsum2[:, m:m + 1],
                                       ALU.mult, ALU.mult).then_inc(weighted, 1)
        if m % G == G - 1:
            nc.vector.reciprocal(rsum[:, m - G + 1:m + 1], sums[:, m - G + 1:m + 1, 0]).then_inc(inverted, 1)

    def combine(dve, i, u):
        if is_first(i) and u == 0:
            return
        m = (u - 1) % UNITS
        n = UNITS * i + u - 1
        dve.wait_ge(weighted, n + 1)
        if not (is_first(i) and u < 3):
            dve.wait_ge(flipped, 2 * (n - 1))
        nc.vector.scalar_tensor_tensor(mix[:, m % 2, :], e[:, 1, m % 2, :], coef[:, m:m + 1], e[:, 0, m % 2, :],
                                       ALU.mult, ALU.add).then_inc(combined, 1)

    def scale_o(dve, i, q, qn):
        dve.wait_ge(pv_done, qn + 1)
        dve.wait_ge(rT_ready, qn + 1)
        if not (is_first(i) and q < 2):
            dve.wait_ge(stored[q % 2], 16 * (qn // 2) if isinstance(qn, int) else 16 * (QT // 2) * (i if q < 3 else i - 1) + 16 * (q // 2))
        nc.vector.tensor_tensor(o_out[:, q % 2, :], pv_bank, rT[:], ALU.mult).then_inc(o_ready, 1)

    def replicate(pool, qn, q):
        pool.wait_ge(inverted, qn + 1)
        if not (isinstance(qn, int) and qn == 0):
            pool.wait_ge(rep_flipped, qn)
        nc.gpsimd.tensor_tensor(rep[:], rsum[:, q * G:(q + 1) * G].unsqueeze(2).to_broadcast([P, G, DH]),
                                ones[:].rearrange("p (h d) -> p h d", d=DH), ALU.mult).then_inc(rep_ready, 1)

    def scores(pe, i, u, a):
        q, h = divmod(u, G)
        n = UNITS * i + u
        if q == 0 and a == 0:
            pe.wait_ge(stack_in[h], 16 * 12 * i + 16 * 12)
        if not (is_first(i) and u == 0):
            pe.wait_ge(exped[a], n)
        for kb in range(S // 512):
            last = nc.tensor.matmul(score_bank[a][:, kb, :], q_st[:, h, a, q * P:(q + 1) * P],
                                    k_st[:, h, a, kb * 512:(kb + 1) * 512], start=True, stop=True)
        last.then_inc(scored[a], 1)

    def flip(pe, i, u, t):
        if is_first(i) and u < 2:
            return
        m = (u - 2) % UNITS
        n = UNITS * i + u - 2
        if t == 0:
            pe.wait_ge(combined, n + 1)
        if not (is_first(i) and u == 2):
            pe.wait_ge(evacuated, 2 * (n - 1) + t + 1)
        for c in range(4):
            last = nc.tensor.transpose(flip_bank[t][:, c * P:(c + 1) * P],
                                       mix[:, m % 2, (4 * t + c) * P:(4 * t + c + 1) * P], ident[:])
        last.then_inc(flipped, 1)

    def values(pe, qn, q, i, half):
        if half == 0:
            pe.wait_ge(evacuated, 2 * G * (qn + 1))
            pe.wait_ge(v_in, 16 * i + 16)
        for c in range(half * SC // 2, (half + 1) * SC // 2):
            for h in range(G):
                last = nc.tensor.matmul(pv_bank[h * DH:(h + 1) * DH, :], v_st[:, c, h * DH:(h + 1) * DH],
                                        mixT[:, q % 2, c, h, :], start=c == 0, stop=c == SC - 1)
        if half:
            last.then_inc(pv_done, 1)
            pe.wait_ge(rep_ready, qn + 1)
            nc.tensor.transpose(r_bank, rep[:].rearrange("p h d -> p (h d)"), ident[:]).then_inc(rep_flipped, 1)

    def is_tile_first(i):
        return isinstance(i, int) and i == F0

    def values_job(pe, i, u, side, half):
        q = PV_SLOT[side][u]
        if q == 3 and is_first(i):
            return
        if half == 0:
            if side == "project" and u > 2:
                pe.wait_ge(proj.got_lo, NJOB * (i + NG) + JOB_SLOT[u - 2] + 1)
            elif side == "feed" and u == 3:
                pe.wait_ge(ffn.step1, 3 * (i - F0) + 1)
            elif side == "feed" and u > 6:
                pe.wait_ge(ffn.gate_ok, GATES * (i - F0) + GATE_SLOT[u - 2] + 1)
            elif side == "feed":
                pe.wait_ge(o_ready, QT * i)
            else:
                pe.wait_ge(o_ready, QT * i - 1)
        if q == 3:
            values(pe, QT * i - 1, 3, i - 1, half)
        else:
            values(pe, QT * i + q, q, i, half)

    def projection_job(pe, i, u, half):
        k = JOB_SLOT[u]
        if half == 0:
            if u % 2 == 0 and not (is_first(i) and u == 4):
                pe.wait_ge(o_ready, QT * i + u // 4 - 1)
            pe.wait_ge(proj.got_lo, NJOB * (i + NG) + sum(v <= u - 2 for v in JOB_SLOT))
            if is_first(i) and k == 0:
                pe.wait_ge(proj.x_lo_dve, 4)
                pe.wait_ge(proj.x_lo_pool, 4)
        proj.multiply(pe, i + NG, k, SIDE + u % 2, (half,))

    def feed_job(pe, i, u, half):
        t = i - F0
        if u == 0 and not is_tile_first(i):
            ffn.back(pe, t - 1, SIDE + 1, 2 + half)
        if u == 1:
            if half == 0:
                pe.wait_ge(o_ready, QT * i - 1)
                if is_tile_first(i):
                    pe.wait_ge(proj.got_lo, 2 * NG * NJOB)
                    pe.wait_ge(ffn.wo_in, 32)
            ffn.project(pe, t, SIDE, half)
        if u == 4 and half == 0:
            if not is_tile_first(i):
                pe.wait_ge(ffn.step2, 3 * (t - 1) + 1)
            ffn.flip(pe, t, SIDE + 1)
        if u in GATE_SLOT:
            if half == 0:
                g = sum(v <= u - 2 for v in GATE_SLOT)
                if g:
                    pe.wait_ge(ffn.gate_ok, GATES * t + g)
                elif is_tile_first(i) and u == 7:
                    pe.wait_ge(ffn.w13_in, 32)
                if u % 2 == 0:
                    pe.wait_ge(o_ready, QT * i + u // 4 - 1)
            ffn.hidden_pair(pe, t, GATE_SLOT[u], SIDE + u % 2, half)
        if u == UNITS - 1:
            if half == 0:
                pe.wait_ge(ffn.gate_ok, GATES * t + GATES)
                if is_tile_first(i):
                    pe.wait_ge(ffn.w2_in, 16)
            ffn.back(pe, t, SIDE + 1, half)

    def side_job(pe, i, u, side, half):
        if u in PV_SLOT[side]:
            values_job(pe, i, u, side, half)
        if side == "project" and u in JOB_SLOT:
            projection_job(pe, i, u, half)
        if side == "feed":
            feed_job(pe, i, u, half)

    def tensor_step(pe, i, side):
        for u in range(UNITS):
            scores(pe, i, u, 0)
            flip(pe, i, u, 0)
            scores(pe, i, u, 1)
            flip(pe, i, u, 1)
            side_job(pe, i, u, side, 0)
            side_job(pe, i, u, side, 1)

    def scalar_step(act, i, side):
        for u in range(UNITS):
            if u - 1 in PV_SLOT[side]:
                q = PV_SLOT[side][u - 1]
                if q < 3:
                    take_r(act, QT * i + q, is_first(i) and q == 0)
                elif not is_first(i):
                    take_r(act, QT * i - 1, False)
            if side == "project":
                if is_first(i) and u < 2:
                    for c in (2 * u, 2 * u + 1):
                        proj.split_x_hi(act, 1, c)
                if u == 1:
                    proj.split_w_hi(act, i + NG, False)
                if u - 1 in JOB_SLOT:
                    proj.take_hi(act, i + NG, JOB_SLOT[u - 1], SIDE + (u - 1) % 2, False)
            if side == "feed":
                t = i - F0
                if u == 0:
                    ffn.split_hi(act, t)
                if u == 5:
                    ffn.y_parts_hi(act, t, SIDE + 1)
                if u - 1 in GATE_SLOT:
                    ffn.tanh(act, t, GATE_SLOT[u - 1], SIDE + (u - 1) % 2)
                if u - 2 in GATE_SLOT:
                    ffn.gate_hi(act, t, GATE_SLOT[u - 2])
            for half in range(2):
                exponentials(act, i, u, half)
                evacuate(act, i, u, half)
        if side == "project":
            proj.take_hi(act, i + NG, NJOB - 1, SIDE + 1, False)

    def vector_step(dve, i, side):
        for u in range(UNITS):
            maximum(dve, i, u, 0)
            weigh(dve, i, u)
            maximum(dve, i, u, 1)
            combine(dve, i, u)
            if u - 1 in PV_SLOT[side]:
                q = PV_SLOT[side][u - 1]
                if q < 3:
                    scale_o(dve, i, q, QT * i + q)
                elif not is_first(i):
                    scale_o(dve, i, q, QT * i - 1)
            if side == "project":
                if is_first(i) and u in (1, 2):
                    proj.split_x_lo(dve, nc.vector, 1, u - 1, proj.x_lo_dve)
                if u - 1 in JOB_SLOT:
                    proj.take_lo(dve, i + NG, JOB_SLOT[u - 1], SIDE + (u - 1) % 2)
            if side == "feed":
                t = i - F0
                if u == 1 and not is_tile_first(i):
                    ffn.residual2(dve, t - 1, SIDE + 1)
                if u == 2:
                    ffn.residual(dve, t, SIDE)
                    if not is_tile_first(i):
                        ffn.norm2(dve, t - 1)
                if u == 3:
                    ffn.norm1(dve, t)
                if u == 5:
                    ffn.y_parts_lo(dve, t, SIDE + 1)
                if u - 1 in GATE_SLOT:
                    ffn.gate(dve, t, GATE_SLOT[u - 1], SIDE + (u - 1) % 2)
        if side == "project":
            proj.take_lo(dve, i + NG, NJOB - 1, SIDE + 1)

    def gpsimd_step(pool, i, side):
        if not is_first(i):
            pool.wait_ge(weighted, UNITS * i)
        nc.gpsimd.tensor_tensor(nlam4[:], nlam[:, bass.ds(i * G, G)], ones[:, 0:G], ALU.mult).then_inc(lam_step, 1)
        if not is_first(i):
            replicate(pool, QT * i - 1, 3)
        if side == "feed":
            if is_tile_first(i):
                pool.wait_ge(ffn.x_in, 32)
                nc.gpsimd.memset(ffn.expo[:], -0.5).then_inc(ffn.expo_ok, 1)
                pool.wait_ge(ffn.expo_ok, 1)
            ffn.split_lo(pool, i - F0)
        for u in range(UNITS):
            if side == "project":
                if is_first(i) and u in (0, 1):
                    proj.split_x_lo(pool, nc.gpsimd, 1, u + 2, proj.x_lo_pool)
                if 1 <= u <= NW:
                    proj.split_w_lo(pool, i + NG, u - 1)
            if u and u % G == 0:
                replicate(pool, QT * i + u // G - 1, u // G - 1)
            if side == "feed":
                t = i - F0
                if u == 1 and not is_tile_first(i):
                    ffn.power(pool, t - 1, 1, ffn.stat2, ffn.pow2)
                if u == 2:
                    ffn.power(pool, t, 0, ffn.stat1, ffn.pow1)
                if u - 2 in GATE_SLOT:
                    ffn.gate_lo(pool, t, GATE_SLOT[u - 2])

    def sync_step(sp, i, side, last=False):
        if side == "project" and not is_first(i):
            proj.load_w(sp, i + NG, False)
        if side == "feed" and is_tile_first(i):
            sp.wait_ge(proj.product, 2 * NG * NJOB)
            sp.wait_ge(proj.w_lo_ok, 2 * NG * NW)
            sp.wait_ge(proj.got_lo, 2 * NG * NJOB)
            for s in proj.stored:
                sp.wait_ge(s, 2 * NG * NJOB * 16)
            ffn.load(sp, 0)
            ffn.load_weights(sp)
        for u in range(UNITS):
            if u - 1 in PV_SLOT[side]:
                q = PV_SLOT[side][u - 1]
                if q < 3:
                    store_o(sp, i, q)
                elif not is_first(i):
                    store_o(sp, i - 1, 3)
                if q == 3:
                    load_v(sp, i)
                    if side == "feed" and not is_tile_first(i):
                        ffn.store(sp, i - F0 - 1)
            if side == "project" and u - 2 in JOB_SLOT:
                proj.store(sp, i + NG, 1, JOB_SLOT[u - 2])
            if side == "feed" and u == 10:
                if not is_tile_first(i):
                    sp.wait_ge(ffn.stored, 16 * (i - F0))
                sp.wait_ge(ffn.step1, 3 * (i - F0) + 1)
                sp.wait_ge(stored[0], 16 * 2 * i + 16)
                sp.wait_ge(stored[1], 16 * 2 * i)
                ffn.load(sp, i - F0 + 1)
            if u >= UNITS - G + 1 and not last:
                h = u - (UNITS - G + 1)
                sp.wait_ge(scored[1], UNITS * i + UNITS - G + h + 1)
                load_stack(sp, i + 1, h)
        if side == "project":
            proj.store(sp, i + NG, 1, NJOB - 1)
        if not last:
            sp.wait_ge(scored[1], UNITS * i + UNITS)
            load_stack(sp, i + 1, G - 1)

    def every_step(eng, step):
        step(eng, 0, "project")
        with eng.Fori(1, NG) as i:
            step(eng, i, "project")
        step(eng, F0, "feed")
        with eng.Fori(F0 + 1, NSTEP) as i:
            step(eng, i, "feed")

    QL = QT * NSTEP - 1
    TL = NTILE - 1

    with nc.Block() as block:
        @block.sync
        def _(sp):
            sp.dma_start(lam_raw[:], lam.partition_broadcast(P)).then_inc(lam_in, 16)
            for s in proj.stored:
                sp.wait_ge(s, NG * NJOB * 16)
            for h in range(G):
                load_stack(sp, 0, h)
            sync_step(sp, 0, "project")
            with sp.Fori(1, NG) as i:
                sync_step(sp, i, "project")
            sync_step(sp, F0, "feed")
            with sp.Fori(F0 + 1, NSTEP - 1) as i:
                sync_step(sp, i, "feed")
            sync_step(sp, NSTEP - 1, "feed", last=True)
            store_o(sp, NSTEP - 1, 3)
            ffn.store(sp, TL)
            sp.wait_ge(ffn.stored, 16 * NTILE)
            for half in range(2):
                sp.wait_ge(stored[half], 16 * 2 * NSTEP)
            sp.wait_ge(ffn.x_in, 32 * (NTILE + 1))

        @block.gpsimd
        def _(pool):
            pool.wait_ge(lam_in, 16)
            for r in range(NSTEP * G // H):
                last = nc.gpsimd.tensor_scalar(nlam[:, r * H:(r + 1) * H], lam_raw[:], -1.0, 1.0, ALU.mult, ALU.mult)
            last.then_inc(lam_step, 1)
            pool.wait_ge(lam_step, 1)
            every_step(pool, gpsimd_step)
            replicate(pool, QL, 3)
            ffn.power(pool, TL, 1, ffn.stat2, ffn.pow2)

        @block.scalar
        def _(act):
            every_step(act, scalar_step)
            for u in range(2):
                for half in range(2):
                    evacuate(act, NSTEP, u, half)
            take_r(act, QL, False)

        @block.vector
        def _(dve):
            every_step(dve, vector_step)
            weigh(dve, NSTEP, 0)
            combine(dve, NSTEP, 0)
            scale_o(dve, NSTEP, 3, QL)
            ffn.residual2(dve, TL, SIDE + 1)
            ffn.norm2(dve, TL)

        @block.tensor
        def _(pe):
            every_step(pe, tensor_step)
            for piece in (2, 3):
                ffn.back(pe, TL, SIDE + 1, piece)
            for u in range(2):
                for half in range(2):
                    flip(pe, NSTEP, u, half)
            pe.wait_ge(o_ready, QL)
            for half in range(2):
                values(pe, QL, 3, NSTEP - 1, half)


def last_block(nc, ctx, x, oT, ffn, facs, ident, out, psum):
    w13, w2, wo_hi, wo_lo = ffn.w13, ffn.w2, ffn.wo_hi, ffn.wo_lo
    sb, sem = scopes(nc, ctx)
    TT = QB // P
    T0 = T - QB
    o_raw = sb("l_o_raw", [P, KC, QB], F32)
    o_hi = sb("l_o_hi", [P, KC, QB], F32R)
    o_lo = sb("l_o_lo", [P, KC, QB], F32R)
    res = sb("l_res", [P, TT, D], F32)
    y = sb("l_y", [P, TT, D], F32)
    z = sb("l_z", [P, TT, D], F32)
    stats = sb("l_stats", [P, TT, 6], F32)
    pause = sb("l_pause", [P, 1], F32)
    mv = sb("l_mv", [P, 2, TT, 2], F32)
    rstd = sb("l_rstd", [P, 2, TT], F32)
    consts = sb("l_consts", [P, 1], F32)
    y_hi = sb("l_y_hi", [P, KC, QB], F16)
    y_lo = sb("l_y_lo", [P, KC, QB], F16)
    th = sb("l_th", [P, 2, QB], F32)
    gated = sb("l_gated", [P, 2, QB], F32)
    g_hi = sb("l_g_hi", [P, FC, QB], F16)
    g_lo = sb("l_g_lo", [P, FC, QB], F16)
    (x_in, o_hi_ok, o_lo_ok, projected, stat, powed, normed, dve_step, flipped, y_hi_ok, y_lo_ok,
     hidden, tanhed, gate_ok, g_hi_ok, g_lo_ok, down, stored, const_ok, hidden_used) = (sem("l_" + n) for n in (
         "x_in", "o_hi_ok", "o_lo_ok", "projected", "stat", "powed", "normed", "dve_step",
         "flipped", "y_hi_ok", "y_lo_ok", "hidden", "tanhed", "gate_ok", "g_hi_ok", "g_lo_ok", "down", "stored", "const_ok", "hidden_used"))

    with nc.Block() as block:
        @block.sync
        def _(sp):
            sp.dma_start(o_raw[:], oT[:, T0:T].rearrange("(c p) t -> p c t", p=P)).then_inc(x_in, 16)
            sp.dma_start(res[:], x[T0:T, :].rearrange("(c p) d -> p c d", p=P)).then_inc(x_in, 16)
            for tt in range(TT):
                sp.wait_ge(normed, TT + tt + 1)
                sp.dma_start(out[T0 + tt * P:T0 + (tt + 1) * P, :], z[:, tt, :]).then_inc(stored, 16)
            sp.wait_ge(stored, 16 * TT)

        @block.gpsimd
        def _(pool):
            nc.gpsimd.memset(consts[:], -0.5).then_inc(const_ok, 1)
            pool.wait_ge(const_ok, 1)
            for ln in range(2):
                for tt in range(TT):
                    pool.wait_ge(stat, TT * ln + tt + 1)
                    nc.gpsimd.tensor_tensor(rstd[:, ln, tt:tt + 1], mv[:, ln, tt, 1:2], consts[:], ALU.pow).then_inc(powed, 1)
                if ln == 0:
                    for f in range(FC):
                        pool.wait_ge(g_hi_ok, f + 1)
                        nc.gpsimd.tensor_tensor(g_lo[:, f, :], gated[:, f % 2, :], g_hi[:, f, :], ALU.subtract).then_inc(g_lo_ok, 1)

        def gate_copy(act, f):
            act.wait_ge(gate_ok, f + 1)
            nc.scalar.activation(g_hi[:, f, :], gated[:, f % 2, :], ACT.Copy).then_inc(g_hi_ok, 1)

        @block.scalar
        def _(act):
            act.wait_ge(x_in, 32)
            nc.scalar.activation(o_hi[:].rearrange("p c d -> p (c d)"), o_raw[:].rearrange("p c d -> p (c d)"), ACT.Copy).then_inc(o_hi_ok, 1)
            for c in range(KC):
                act.wait_ge(flipped, c + 1)
                nc.scalar.activation(y_hi[:, c, :], psum[:, c % 2, :], ACT.Copy, scale=XSCALE).then_inc(y_hi_ok, 1)
            for f in range(FC):
                act.wait_ge(hidden, 2 * f + 1)
                if f >= 2:
                    act.wait_ge(gate_ok, f - 1)
                nc.scalar.activation(th[:, f % 2, :], psum[:, 2 + 2 * (f % 2), :], ACT.Tanh, scale=facs[:, 0:1]).then_inc(tanhed, 1)
                if f >= 1:
                    gate_copy(act, f - 1)
            gate_copy(act, FC - 1)

        @block.vector
        def _(dve):
            def moments(ln, tt, base, count):
                dve.wait_ge(dve_step, base + 1)
                nc.vector.bn_stats(stats[:, tt, :], z[:, tt, :]).then_inc(dve_step, 1)
                dve.wait_ge(dve_step, base + 2)
                nc.vector.memset(pause[:], 0.0)
                nc.vector.bn_aggr(mv[:, ln, tt, :], stats[:, tt, :]).then_inc(dve_step, 1)
                dve.wait_ge(dve_step, base + 3)
                nc.vector.tensor_scalar(mv[:, ln, tt, 1:2], mv[:, ln, tt, 1:2], EPS, None, ALU.add).then_inc(stat, 1)

            def normalise(ln, tt, dst, count):
                dve.wait_ge(powed, count)
                nc.vector.tensor_scalar(dst, z[:, tt, :], mv[:, ln, tt, 0:1], rstd[:, ln, tt:tt + 1], ALU.subtract,
                                        ALU.mult).then_inc(normed, 1)
            dve.wait_ge(o_hi_ok, 1)
            nc.vector.tensor_tensor(o_lo[:], o_raw[:], o_hi[:].bitcast(F32), ALU.subtract).then_inc(o_lo_ok, 1)
            for tt in range(TT):
                dve.wait_ge(projected, tt + 1)
                nc.vector.tensor_tensor(z[:, tt, :], psum[:, 6 + tt % 2, :], res[:, tt, :], ALU.add).then_inc(dve_step, 1)
                moments(0, tt, 3 * tt, 0)
                if tt:
                    normalise(0, tt - 1, y[:, tt - 1, :], tt)
            normalise(0, TT - 1, y[:, TT - 1, :], TT)
            for c in range(KC):
                dve.wait_ge(y_hi_ok, c + 1)
                nc.vector.scalar_tensor_tensor(y_lo[:, c, :], psum[:, c % 2, :], XSCALE, y_hi[:, c, :], ALU.mult,
                                               ALU.subtract).then_inc(y_lo_ok, 1)
            for f in range(FC):
                dve.wait_ge(tanhed, f + 1)
                if f >= 2:
                    dve.wait_ge(g_lo_ok, f - 1)
                nc.vector.scalar_tensor_tensor(gated[:, f % 2, :], th[:, f % 2, :], 1.0, psum[:, 2 + 2 * (f % 2), :],
                                               ALU.add, ALU.mult).then_inc(hidden_used, 1)
                dve.wait_ge(hidden, 2 * f + 2)
                dve.wait_ge(hidden_used, f + 1)
                nc.vector.scalar_tensor_tensor(gated[:, f % 2, :], gated[:, f % 2, :], GSCALE, psum[:, 3 + 2 * (f % 2), :],
                                               ALU.mult, ALU.mult).then_inc(gate_ok, 1)
            for tt in range(TT):
                dve.wait_ge(down, tt + 1)
                nc.vector.scalar_tensor_tensor(z[:, tt, :], psum[:, 6 + tt % 2, :], facs[:, 1:2], y[:, tt, :], ALU.mult,
                                               ALU.add).then_inc(dve_step, 1)
                moments(1, tt, 3 * (TT + tt), 0)
                if tt:
                    normalise(1, tt - 1, z[:, tt - 1, :], TT + tt)
            normalise(1, TT - 1, z[:, TT - 1, :], 2 * TT)

        @block.tensor
        def _(pe):
            pe.wait_ge(o_lo_ok, 1)
            for tt in range(TT):
                if tt >= 2:
                    pe.wait_ge(dve_step, 3 * (tt - 2) + 1)
                n = 0
                for op, wp in ((o_hi, wo_hi), (o_hi, wo_lo), (o_lo, wo_hi)):
                    for c in range(KC):
                        last = nc.tensor.matmul(psum[:, 6 + tt % 2, :], op[:, c, tt * P:(tt + 1) * P], wp[:, c, :],
                                                start=n == 0, stop=n == 3 * KC - 1)
                        n += 1
                last.then_inc(projected, 1)
            pe.wait_ge(normed, TT)
            for c in range(KC):
                if c >= 2:
                    pe.wait_ge(y_lo_ok, c - 1)
                for tt in range(TT):
                    last = nc.tensor.transpose(psum[:, c % 2, tt * P:(tt + 1) * P], y[:, tt, c * P:(c + 1) * P], ident[:])
                last.then_inc(flipped, 1)
            pe.wait_ge(y_lo_ok, KC)
            for f in range(FC):
                if f >= 2:
                    pe.wait_ge(gate_ok, f - 1)
                for m in range(2):
                    n = 0
                    for part in (y_hi, y_lo):
                        for c in range(KC):
                            last = nc.tensor.matmul(psum[:, 2 + m + 2 * (f % 2), :], w13[:, m, c, f * P:(f + 1) * P],
                                                    part[:, c, :], start=n == 0, stop=n == 2 * KC - 1)
                            n += 1
                    last.then_inc(hidden, 1)
            pe.wait_ge(g_lo_ok, FC)
            for tt in range(TT):
                if tt >= 2:
                    pe.wait_ge(dve_step, 3 * (TT + tt - 2) + 1)
                n = 0
                for part in (g_hi, g_lo):
                    for f in range(FC):
                        last = nc.tensor.matmul(psum[:, 6 + tt % 2, :], part[:, f, tt * P:(tt + 1) * P], w2[:, f, :],
                                                start=n == 0, stop=n == 2 * FC - 1)
                        n += 1
                last.then_inc(down, 1)


def build(nc, x, xT, w5, woT, lam, wff, out):
    qk = nc.dram_tensor("qk_parts", [B, MATS, 2, D, S], F32, kind="Internal").ap()
    vs = nc.dram_tensor("v_rows", [B, S, D], F32, kind="Internal").ap()
    oT = nc.dram_tensor("o_T", [D, T], F32, kind="Internal").ap()
    wq = nc.dram_tensor("w_ternary", [3, P, KC * HP], F16, kind="Internal").ap()
    wod = nc.dram_tensor("wo_parts", [2, P, KC * D], F32, kind="Internal").ap()
    with ExitStack() as whole:
        sb, sem = scopes(nc, whole)
        psum = whole.enter_context(nc.psum_tensor("psum", [P, 8, 512], F32))
        facs = sb("facs", [P, 2], F32)
        ident = sb("ident", [P, P], F32)
        ones = sb("ones", [P, P], F32)
        id_ok = sem("id_ok")
        with nc.Block() as block:
            @block.gpsimd
            def _(pool):
                nc.gpsimd.memset(ident[:], 0.0).then_inc(id_ok, 1)
                pool.wait_ge(id_ok, 1)
                nc.gpsimd.affine_select(out=ident[:], in_=ident[:], compare_op=ALU.not_equal, fill=1.0, base=0,
                                        pattern=[[-1, P]], channel_multiplier=1).then_inc(id_ok, 1)
        sems = whole.enter_context(ExitStack())
        with ExitStack() as region:
            proj = Projections(nc, region, sems, xT, w5, qk, vs, psum)
            with ExitStack() as ctx:
                prepare(nc, ctx, proj, wff, woT, wq, wod, facs, ones)
        with ExitStack() as region:
            ffn = FeedForward(nc, region, sems, x, oT, wq, wod, facs, ident, out, psum)
            with nc.sbuf_tensor("filler", [P, max(0, proj.size - ffn.size) // 4], F32), ExitStack() as ctx:
                attention(nc, ctx, lam, qk, vs, oT, ones, ident, psum, proj, ffn)
            with ExitStack() as ctx:
                last_block(nc, ctx, x, oT, ffn, facs, ident, out, psum)


def kernel(**inputs):
    import numpy as np
    import concourse.bacc as bacc
    from concourse.bass_utils import run_bass_kernel_spmd as run

    a = {k.replace("L0_", ""): np.asarray(v) for k, v in inputs.items()}

    def padded(w, shape):
        out = np.zeros(shape, w.dtype)
        out[tuple(slice(0, n) for n in w.shape)] = w
        return out

    def on_partitions(w):
        return w.reshape(-1, P, w.shape[1]).transpose(1, 0, 2).reshape(P, -1)

    wT = np.stack([a[f"attn_{n}_w"].T for n in ("q1", "k1", "q2", "k2", "v")])
    laid = {
        "x": a["attn_x"].reshape(T, D),
        "xT": a["attn_x"].transpose(0, 2, 1),
        "w5": wT.reshape(NW, KC, P, NG, P).transpose(3, 2, 0, 1, 4).reshape(NG, P, NW * KC * P),
        "woT": a["attn_o_w"].T,
        "lam": a["attn_lambda_param"],
        "wff": np.stack([on_partitions(padded(a["ffn_w2"].T, (HP, D))),
                         on_partitions(padded(a["ffn_w3"].T, (D, HP))),
                         on_partitions(padded(a["ffn_w1"].T, (D, HP)))]),
    }
    laid = {k: np.ascontiguousarray(v) for k, v in laid.items()}
    nc = bacc.Bacc("TRN2", target_bir_lowering=False, num_devices=1)
    args = [nc.dram_tensor(f"in_{k}", v.shape, mybir.dt.from_np(v.dtype), kind="ExternalInput").ap() for k, v in laid.items()]
    out = nc.dram_tensor("out", (T, D), F32, kind="ExternalOutput").ap()
    build(nc, *args, out)
    r = run(nc, [{f"in_{k}": v for k, v in laid.items()}], core_ids=[0])
    return r.results[0]["out"].reshape(B, S, D)
```

```python
from contextlib import ExitStack

import concourse.bass as bass
from concourse import mybir

F32 = mybir.dt.float32
F32R = mybir.dt.float32r
F16 = mybir.dt.float16
ALU = mybir.AluOpType
ACT = mybir.ActivationFunctionType
AX = mybir.AxisListType

P = 128
B, S, D = 2, 1024, 512
H, DH = 16, 32
HIDDEN = int(2 * D * 4 / 3)
T = B * S
KC = D // P
FC = -(-HIDDEN // P)
HP = FC * P
G = P // DH
NG = H // G
QB = 512
NQB = S // QB
SC = S // P
QT = QB // P
UNITS = QT * G
NSTEP = B * NQB * NG
MATS = 4
NW = MATS + 1
EPS = 1e-5
SCORE_SCALE = float(DH) ** -0.5
XSCALE = 1024.0
GSCALE = 2.0 ** -24


def scopes(nc, ctx, sems=None):
    def sb(name, shape, dt):
        return ctx.enter_context(nc.sbuf_tensor(name, shape, dt))

    def sem(name):
        return (sems or ctx).enter_context(nc.semaphore(name))
    return sb, sem


SIDE = 6
PV_SLOT = {2: 3, 6: 0, 10: 1, 14: 2}
JOB_SLOT = {u: k for k, u in enumerate((3, 4, 5, 7, 8, 9, 11, 12, 13, 15))}
NJOB = len(JOB_SLOT)
JOBS = [("v", MATS, tb) for tb in range(S // 512)] + [("qk", m, tb) for m in range(MATS) for tb in range(S // 512)]
VW = 640
GATES = -(-FC // 2)
GATE_SLOT = {u: k for k, u in enumerate((5, 7, 8, 9, 11, 12))}
F0 = NG
NTILE = NSTEP - F0


class Projections:

    X_RAW = 4 * (NW + 2 * MATS + 1) * KC * P

    def __init__(self, nc, ctx, sems, xT, w5, qk, vs, psum):
        self.nc, self.xT, self.w5, self.qk, self.vs, self.psum = nc, xT, w5, qk, vs, psum
        sb, sem = scopes(nc, ctx, sems)
        self.w_raw = sb("p_w_raw", [P, NW, KC, P], F32)
        self.w_hi = sb("p_w_hi", [P, MATS, KC, P], F32R)
        self.w_lo = sb("p_w_lo", [P, MATS, KC, P], F32R)
        self.w_v = sb("p_w_v", [P, KC, P], F32)
        self.x_raw = sb("p_x_raw", [P, KC, S], F32)
        self.x_hi = sb("p_x_hi", [P, KC, S], F32R)
        self.x_lo = sb("p_x_lo", [P, KC, S], F32R)
        self.out_hi = sb("p_out_hi", [P, 2, 512], F32R)
        self.out_lo = sb("p_out_lo", [P, 2, 512], F32R)
        self.out_v = sb("p_out_v", [P, 2, 512], F32)
        self.size = 4 * ((3 * MATS + 2) * KC * P + 3 * KC * S + 3 * 2 * 512)
        self.x_in = [sem(f"p_x_in{c}") for c in range(KC)]
        self.w_in, self.w_hi_ok, self.w_lo_ok, self.x_hi_ok, self.x_lo_dve, self.x_lo_pool = (
            sem("p_" + n) for n in ("w_in", "w_hi_ok", "w_lo_ok", "x_hi_ok", "x_lo_dve", "x_lo_pool"))
        self.product, self.got_hi, self.got_lo = (sem("p_" + n) for n in ("product", "got_hi", "got_lo"))
        self.stored = [sem(f"p_stored{i}") for i in range(2)]

    def load_x(self, sp, b):
        if b:
            sp.wait_ge(self.product, NJOB * NG * b)
        for c in range(KC):
            sp.dma_start(self.x_raw[:, c, :], self.xT[b, c * P:(c + 1) * P, :]).then_inc(self.x_in[c], 16)

    def load_w(self, sp, j, first):
        if not first:
            sp.wait_ge(self.w_lo_ok, MATS * j)
        sp.dma_start(self.w_raw[:].rearrange("p m c f -> p (m c f)"),
                     self.w5[bass.ds(j % NG, 1)].rearrange("a p n -> p (a n)")).then_inc(self.w_in, 16)

    def split_x_hi(self, act, b, c):
        act.wait_ge(self.x_in[c], 16 * (b + 1))
        if b:
            act.wait_ge(self.product, NJOB * NG * b)
        self.nc.scalar.activation(self.x_hi[:, c, :], self.x_raw[:, c, :], ACT.Copy).then_inc(self.x_hi_ok, 1)

    def split_x_lo(self, eng, vector, b, c, done):
        eng.wait_ge(self.x_hi_ok, KC * b + c + 1)
        vector.tensor_tensor(self.x_lo[:, c, :], self.x_raw[:, c, :], self.x_hi[:, c, :].bitcast(F32),
                             ALU.subtract).then_inc(done, 1)

    def split_w_hi(self, act, j, turn, first):
        m = (turn - 1) % NW
        act.wait_ge(self.w_in, 16 * j + 16)
        if not first:
            act.wait_ge(self.product, NJOB * (j - 1) + 2 * turn + 2)
        dst = self.w_hi[:, m] if m < MATS else self.w_v[:]
        self.nc.scalar.activation(dst.rearrange("p c f -> p (c f)"),
                                  self.w_raw[:, m].rearrange("p c f -> p (c f)"), ACT.Copy).then_inc(self.w_hi_ok, 1)

    def split_w_lo(self, pool, j, m):
        pool.wait_ge(self.w_hi_ok, NW * j + m + 2)
        self.nc.gpsimd.tensor_tensor(self.w_lo[:, m].rearrange("p c f -> p (c f)"),
                                     self.w_raw[:, m].rearrange("p c f -> p (c f)"),
                                     self.w_hi[:, m].rearrange("p c f -> p (c f)").bitcast(F32),
                                     ALU.subtract).then_inc(self.w_lo_ok, 1)

    def multiply(self, pe, j, k, bank, halves=(0, 1)):
        kind, m, tb = JOBS[k]
        nc, ps = self.nc, self.psum[:, bank, :]
        terms = ((self.x_hi, self.w_hi), (self.x_hi, self.w_lo), (self.x_lo, self.w_hi))
        if kind == "qk":
            if 0 in halves:
                pe.wait_ge(self.w_lo_ok, MATS * j + m + 1)
            products = [(ps, wp[:, m, c, :], xp[:, c, tb * 512:(tb + 1) * 512], n == c == 0, n == 2 and c == KC - 1)
                        for n, (xp, wp) in enumerate(terms) for c in range(KC)]
        else:
            if 0 in halves:
                pe.wait_ge(self.w_hi_ok, NW * j + 1)
            products = [(ps[:, q * P:(q + 1) * P], self.x_raw[:, c, tb * 512 + q * P:tb * 512 + (q + 1) * P],
                         self.w_v[:, c, :], c == 0, c == KC - 1) for q in range(4) for c in range(KC)]
        for half in halves:
            for dst, stationary, moving, start, stop in products[half * len(products) // 2:(half + 1) * len(products) // 2]:
                last = nc.tensor.matmul(dst, stationary, moving, start=start, stop=stop)
        if 1 in halves:
            last.then_inc(self.product, 1)

    def take_hi(self, act, j, k, bank, first):
        kind, m, tb = JOBS[k]
        act.wait_ge(self.product, NJOB * j + k + 1)
        if not (first and k < 2):
            act.wait_ge(self.stored[k % 2], (NJOB // 2) * 32 * j + k // 2 * 32)
        if kind == "v":
            self.nc.scalar.activation(self.out_v[:, k % 2, 0:256], self.psum[:, bank, 0:256], ACT.Copy).then_inc(self.got_hi, 1)
        else:
            self.nc.scalar.activation(self.out_hi[:, k % 2, :], self.psum[:, bank, :], ACT.Copy,
                                      scale=SCORE_SCALE if m % 2 == 0 else 1.0).then_inc(self.got_hi, 1)

    def take_lo(self, dve, j, k, bank):
        kind, m, tb = JOBS[k]
        dve.wait_ge(self.got_hi, NJOB * j + k + 1)
        if kind == "v":
            self.nc.vector.tensor_copy(self.out_v[:, k % 2, 256:512], self.psum[:, bank, 256:512]).then_inc(self.got_lo, 1)
        else:
            self.nc.vector.scalar_tensor_tensor(self.out_lo[:, k % 2, :], self.psum[:, bank, :],
                                                SCORE_SCALE if m % 2 == 0 else 1.0,
                                                self.out_hi[:, k % 2, :].bitcast(F32), ALU.mult, ALU.subtract).then_inc(self.got_lo, 1)

    def store(self, sp, j, b, k):
        kind, m, tb = JOBS[k]
        f = (j - NG * b) * P
        f = f if isinstance(f, int) else sp.snap(f)
        sp.wait_ge(self.got_lo, NJOB * j + k + 1)
        if kind == "qk":
            for part, stage in ((1, self.out_lo), (0, self.out_hi)):
                sp.dma_start(self.qk[b, m, part, bass.ds(f, P), tb * 512:(tb + 1) * 512],
                             stage[:, k % 2, :].bitcast(F32)).then_inc(self.stored[k % 2], 16)
        else:
            for c in (1, 0):
                sp.dma_start(self.vs[b, tb * 512 + c * 256:tb * 512 + (c + 1) * 256, bass.ds(f, P)].rearrange("(q p) f -> p q f", p=P),
                             self.out_v[:, k % 2, c * 256:(c + 1) * 256].rearrange("p (q f) -> p q f", q=2)).then_inc(self.stored[k % 2], 16)


class FeedForward:

    def __init__(self, nc, ctx, sems, x, oT, wq, wod, facs, ident, out, psum):
        self.nc, self.x, self.oT, self.wq, self.wod = nc, x, oT, wq, wod
        self.facs, self.ident, self.out, self.psum = facs, ident, out, psum
        sb, sem = scopes(nc, ctx, sems)
        self.w2 = sb("f_w2", [P, FC, D], F16)
        self.o_raw = sb("f_o_raw", [P, KC, P], F32)
        self.o_hi = sb("f_o_hi", [P, KC, P], F32R)
        self.o_lo = sb("f_o_lo", [P, KC, P], F32R)
        self.res = sb("f_res", [P, D], F32)
        self.g_hi = sb("f_g_hi", [P, FC, P], F16)
        self.g_lo = sb("f_g_lo", [P, FC, P], F16)
        self.y = sb("f_y", [P, D], F32)
        self.half_gate = sb("f_half_gate", [P, 256], F32)
        before = 2 * (FC * D + 2 * FC * P) + 4 * (3 * KC * P + 2 * D + 256)
        sb("f_fill", [P, (Projections.X_RAW - before) // 4], F32)
        self.wo_hi = sb("f_wo_hi", [P, KC, D], F32R)
        self.wo_lo = sb("f_wo_lo", [P, KC, D], F32R)
        self.w13 = sb("f_w13", [P, 2, KC, HP], F16)
        self.z = sb("f_z", [P, 2, D], F32)
        self.fin = sb("f_fin", [P, D], F32)
        self.y_hi = sb("f_y_hi", [P, KC, P], F16)
        self.y_lo = sb("f_y_lo", [P, KC, P], F16)
        self.th = sb("f_th", [P, 2, 256], F32)
        self.gated = sb("f_gated", [P, 2, 256], F32)
        self.stats = sb("f_stats", [P, 2, 6], F32)
        self.mv = sb("f_mv", [P, 2, 2], F32)
        self.rstd = sb("f_rstd", [P, 2], F32)
        self.pause = sb("f_pause", [P, 1], F32)
        self.expo = sb("f_expo", [P, 1], F32)
        self.eps = sb("f_eps", [P, 1], F32)
        self.veps = sb("f_veps", [P, 2], F32)
        self.size = (Projections.X_RAW + 4 * 2 * KC * D + 2 * 2 * KC * HP + 4 * (3 * D + 4 * 256) + 2 * 2 * KC * P
                     + 4 * (2 * 6 + 2 * 2 + 2 + 3 + 2))
        self.wo_in = sem("f_wo_in")
        self.w13_in = sem("f_w13_in")
        self.w2_in = sem("f_w2_in")
        self.expo_ok = sem("f_expo_ok")
        self.eps_added = sem("f_eps_added")
        self.x_in = sem("f_x_in")
        self.o_hi_ok = sem("f_o_hi_ok")
        self.o_lo_ok = sem("f_o_lo_ok")
        self.projected = sem("f_projected")
        self.stat1 = sem("f_stat1")
        self.stat2 = sem("f_stat2")
        self.step1 = sem("f_step1")
        self.step2 = sem("f_step2")
        self.pow1 = sem("f_pow1")
        self.pow2 = sem("f_pow2")
        self.y_ok = sem("f_y_ok")
        self.fin_ok = sem("f_fin_ok")
        self.flipped = sem("f_flipped")
        self.y_hi_ok = sem("f_y_hi_ok")
        self.y_lo_ok = sem("f_y_lo_ok")
        self.hidden = sem("f_hidden")
        self.tanhed = sem("f_tanhed")
        self.halved = sem("f_halved")
        self.gate_ok = sem("f_gate_ok")
        self.g_hi_ok = sem("f_g_hi_ok")
        self.g_lo_ok = sem("f_g_lo_ok")
        self.down = sem("f_down")
        self.stored = sem("f_stored")

    def load_wo(self, sp):
        sp.dma_start(self.wo_hi[:].rearrange("p c d -> p (c d)").bitcast(F32), self.wod[0]).then_inc(self.wo_in, 16)
        sp.dma_start(self.wo_lo[:].rearrange("p c d -> p (c d)").bitcast(F32), self.wod[1]).then_inc(self.wo_in, 16)

    def load_weights(self, sp):
        for m, j in ((0, 2), (1, 1)):
            sp.dma_start(self.w13[:, m].rearrange("p c f -> p (c f)"), self.wq[j]).then_inc(self.w13_in, 16)
        sp.dma_start(self.w2[:].rearrange("p c d -> p (c d)"), self.wq[0]).then_inc(self.w2_in, 16)

    def load(self, sp, t):
        sp.dma_start(self.o_raw[:], self.oT[:, bass.ds(t * P, P)].rearrange("(c p) t -> p c t", p=P)).then_inc(self.x_in, 16)
        sp.dma_start(self.res[:], self.x[bass.ds(t * P, P), :]).then_inc(self.x_in, 16)

    def split_hi(self, act, t):
        act.wait_ge(self.x_in, 32 * t + 32)
        self.nc.scalar.activation(self.o_hi[:].rearrange("p c t -> p (c t)"), self.o_raw[:].rearrange("p c t -> p (c t)"),
                                  ACT.Copy).then_inc(self.o_hi_ok, 1)

    def split_lo(self, pool, t):
        pool.wait_ge(self.o_hi_ok, t + 1)
        self.nc.gpsimd.tensor_tensor(self.o_lo[:], self.o_raw[:], self.o_hi[:].bitcast(F32), ALU.subtract).then_inc(self.o_lo_ok, 1)

    def project(self, pe, t, bank, half):
        if half == 0:
            pe.wait_ge(self.o_lo_ok, t + 1)
        products = [(op, wp, c) for op, wp in ((self.o_hi, self.wo_hi), (self.o_hi, self.wo_lo), (self.o_lo, self.wo_hi))
                    for c in range(KC)]
        for n in range(half * 6, half * 6 + 6):
            op, wp, c = products[n]
            last = self.nc.tensor.matmul(self.psum[:, bank, :], op[:, c, :], wp[:, c, :], start=n == 0, stop=n == 3 * KC - 1)
        if half:
            last.then_inc(self.projected, 1)

    def moments(self, dve, t, ln, step, stat):
        dve.wait_ge(step, 2 * t + 1)
        self.nc.vector.bn_stats(self.stats[:, ln, :], self.z[:, ln, :]).then_inc(step, 1)
        dve.wait_ge(step, 2 * t + 2)
        self.nc.vector.memset(self.pause[:], 0.0)
        self.nc.vector.bn_aggr(self.mv[:, ln, :], self.stats[:, ln, :]).then_inc(stat, 1)

    def power(self, pool, t, ln, stat, done, added):
        pool.wait_ge(stat, t + 1)
        self.nc.gpsimd.tensor_tensor(self.veps[:, ln:ln + 1], self.mv[:, ln, 1:2], self.eps[:], ALU.add).then_inc(self.eps_added, 1)
        pool.wait_ge(self.eps_added, added)
        self.nc.gpsimd.tensor_tensor(self.rstd[:, ln:ln + 1], self.veps[:, ln:ln + 1], self.expo[:], ALU.pow).then_inc(done, 1)

    def residual(self, dve, t, bank):
        dve.wait_ge(self.projected, t + 1)
        self.nc.vector.tensor_tensor(self.z[:, 0, :], self.psum[:, bank, :], self.res[:], ALU.add).then_inc(self.step1, 1)
        self.moments(dve, t, 0, self.step1, self.stat1)

    def norm1(self, dve, t):
        dve.wait_ge(self.pow1, t + 1)
        self.nc.vector.tensor_scalar(self.y[:], self.z[:, 0, :], self.mv[:, 0, 0:1], self.rstd[:, 0:1], ALU.subtract,
                                     ALU.mult).then_inc(self.y_ok, 1)

    def flip(self, pe, t, bank):
        pe.wait_ge(self.y_ok, t + 1)
        for c in range(KC):
            last = self.nc.tensor.transpose(self.psum[:, bank, c * P:(c + 1) * P], self.y[:, c * P:(c + 1) * P], self.ident[:])
        last.then_inc(self.flipped, 1)

    def y_parts_hi(self, act, t, bank):
        act.wait_ge(self.flipped, t + 1)
        self.nc.scalar.activation(self.y_hi[:].rearrange("p c t -> p (c t)"), self.psum[:, bank, :], ACT.Copy,
                                  scale=XSCALE).then_inc(self.y_hi_ok, 1)

    def y_parts_lo(self, dve, t, bank):
        dve.wait_ge(self.y_hi_ok, t + 1)
        self.nc.vector.scalar_tensor_tensor(self.y_lo[:].rearrange("p c t -> p (c t)"), self.psum[:, bank, :], XSCALE,
                                            self.y_hi[:].rearrange("p c t -> p (c t)"), ALU.mult, ALU.subtract).then_inc(self.y_lo_ok, 1)

    def gate_width(self, q):
        return min(2, FC - 2 * q) * P

    def hidden_pair(self, pe, t, q, bank, m):
        if q == 0 and m == 0:
            pe.wait_ge(self.y_lo_ok, t + 1)
        for f in range(self.gate_width(q) // P):
            n = 0
            for part in (self.y_hi, self.y_lo):
                for c in range(KC):
                    last = self.nc.tensor.matmul(self.psum[:, bank, m * 256 + f * P:m * 256 + (f + 1) * P],
                                                 self.w13[:, m, c, (2 * q + f) * P:(2 * q + f + 1) * P], part[:, c, :],
                                                 start=n == 0, stop=n == 2 * KC - 1)
                    n += 1
        if m:
            last.then_inc(self.hidden, 1)

    def tanh(self, act, t, q, bank):
        w = self.gate_width(q)
        act.wait_ge(self.hidden, GATES * t + q + 1)
        if q >= 2:
            act.wait_ge(self.halved, GATES * t + q - 1)
        self.nc.scalar.activation(self.th[:, q % 2, 0:w], self.psum[:, bank, 0:w], ACT.Tanh, scale=self.facs[:, 0:1]).then_inc(self.tanhed, 1)

    def gate(self, dve, t, q, bank):
        w = self.gate_width(q)
        dve.wait_ge(self.tanhed, GATES * t + q + 1)
        self.nc.vector.scalar_tensor_tensor(self.half_gate[:, 0:w], self.th[:, q % 2, 0:w], 1.0, self.psum[:, bank, 0:w],
                                            ALU.add, ALU.mult).then_inc(self.halved, 1)

    def gate2(self, dve, t, q, bank):
        w = self.gate_width(q)
        if q >= 2:
            dve.wait_ge(self.g_lo_ok, GATES * t + q - 1)
        dve.wait_ge(self.halved, GATES * t + q + 1)
        self.nc.vector.scalar_tensor_tensor(self.gated[:, q % 2, 0:w], self.half_gate[:, 0:w], GSCALE,
                                            self.psum[:, bank, 256:256 + w], ALU.mult, ALU.mult).then_inc(self.gate_ok, 1)

    def gate_hi(self, act, t, q):
        w = self.gate_width(q)
        act.wait_ge(self.gate_ok, GATES * t + q + 1)
        self.nc.scalar.activation(self.g_hi[:, 2 * q:2 * q + w // P, :].rearrange("p c t -> p (c t)"), self.gated[:, q % 2, 0:w],
                                  ACT.Copy).then_inc(self.g_hi_ok, 1)

    def gate_lo(self, pool, t, q):
        w = self.gate_width(q)
        pool.wait_ge(self.g_hi_ok, GATES * t + q + 1)
        self.nc.gpsimd.tensor_tensor(self.g_lo[:, 2 * q:2 * q + w // P, :].rearrange("p c t -> p (c t)"), self.gated[:, q % 2, 0:w],
                                     self.g_hi[:, 2 * q:2 * q + w // P, :].rearrange("p c t -> p (c t)"), ALU.subtract).then_inc(self.g_lo_ok, 1)

    def back(self, pe, t, bank, piece):
        chunks = range(3 * piece, min(FC, 3 * piece + 3))
        pe.wait_ge(self.g_lo_ok, GATES * t + chunks[-1] // 2 + 1)
        for f in chunks:
            for part in (self.g_hi, self.g_lo):
                last = self.nc.tensor.matmul(self.psum[:, bank, :], part[:, f, :], self.w2[:, f, :],
                                             start=f == 0 and part is self.g_hi, stop=f == FC - 1 and part is self.g_lo)
        if piece == 3:
            last.then_inc(self.down, 1)

    def residual2(self, dve, t, bank):
        dve.wait_ge(self.down, t + 1)
        self.nc.vector.scalar_tensor_tensor(self.z[:, 1, :], self.psum[:, bank, :], self.facs[:, 1:2], self.y[:], ALU.mult,
                                            ALU.add).then_inc(self.step2, 1)
        self.moments(dve, t, 1, self.step2, self.stat2)

    def norm2(self, dve, t):
        dve.wait_ge(self.pow2, t + 1)
        self.nc.vector.tensor_scalar(self.fin[:], self.z[:, 1, :], self.mv[:, 1, 0:1], self.rstd[:, 1:2], ALU.subtract,
                                     ALU.mult).then_inc(self.fin_ok, 1)

    def store(self, sp, t):
        sp.wait_ge(self.fin_ok, t + 1)
        sp.dma_start(self.out[bass.ds(t * P, P), :], self.fin[:]).then_inc(self.stored, 16)


def prepare(nc, ctx, proj, wff, woT, wq, wod, facs, ones):
    sb, sem = scopes(nc, ctx)
    N = KC * HP
    raw = sb("q_raw", [P, 2 * N], F32)
    below = sb("q_below", [P, N], F16)
    tern = sb("q_tern", [P, N], F16)
    part = sb("q_part", [P, 1], F32)
    half = sb("q_half", [P, 2], F32)
    wo_raw = sb("q_wo_raw", [P, KC * D], F32)
    wo_hi = sb("q_wo_hi", [P, KC * D], F32R)
    wo_lo = sb("q_wo_lo", [P, KC * D], F32R)
    raw_in, summed, reduced, halved, compared, ternary, stored, wo_in, wo_hi_ok, wo_lo_ok, ones_ok, facs_ok = (
        sem("q_" + n) for n in ("raw_in", "summed", "reduced", "halved", "compared", "ternary", "stored", "wo_in",
                                "wo_hi_ok", "wo_lo_ok", "ones_ok", "facs_ok"))
    BANKS = 5
    sum_bank = proj.psum[:, 7, 0:1]

    with nc.Block() as block:
        @block.sync
        def _(sp):
            proj.load_w(sp, 0, True)
            proj.load_x(sp, 0)
            sp.dma_start(wo_raw[:].rearrange("p (c d) -> p c d", c=KC), woT.rearrange("(c p) d -> p c d", p=P)).then_inc(wo_in, 16)

            def stores(j, other=None):
                for k in range(NJOB):
                    if k == 2:
                        proj.load_w(sp, j + 1, False)
                    proj.store(sp, j, 0, k)
                    if other is not None:
                        other(k)
            stores(0)
            for n in range(4):
                sp.dma_start(raw[:, n * N // 4:(n + 1) * N // 4], wff[0, :, n * N // 4:(n + 1) * N // 4]).then_inc(raw_in, 16)
            sp.wait_ge(wo_lo_ok, 1)
            sp.dma_start(wod[0], wo_hi[:].bitcast(F32)).then_inc(stored, 16)
            sp.dma_start(wod[1], wo_lo[:].bitcast(F32)).then_inc(stored, 16)
            with sp.Fori(1, NG) as j:
                def ternary_traffic(k):
                    if k == 0:
                        sp.wait_ge(raw_in, 64 * j)
                    if k < 4:
                        sp.dma_start(raw[:, bass.ds((j % 2) * N + k * N // 4, N // 4)],
                                     wff[bass.ds(j % (NG - 1), 1), :, k * N // 4:(k + 1) * N // 4].rearrange("a p n -> p (a n)")).then_inc(raw_in, 16)
                    if k == 8:
                        sp.wait_ge(ternary, j)
                        for n in range(2):
                            sp.dma_start(wq[bass.ds(j - 1, 1), :, n * N // 2:(n + 1) * N // 2].rearrange("a p n -> p (a n)"),
                                         tern[:, n * N // 2:(n + 1) * N // 2]).then_inc(stored, 16)
                stores(j, ternary_traffic)
            sp.wait_ge(stored, 32 * NG)
            sp.wait_ge(raw_in, 64 * NG)

        @block.gpsimd
        def _(pool):
            nc.gpsimd.memset(ones[:], 1.0).then_inc(ones_ok, 1)
            proj.split_w_lo(pool, 0, 0)
            proj.split_x_lo(pool, nc.gpsimd, 0, 3, proj.x_lo_pool)
            for m in range(1, MATS):
                proj.split_w_lo(pool, 0, m)
            with pool.Fori(1, NG + 1) as j:
                for m in range(MATS):
                    proj.split_w_lo(pool, j, m)

        @block.scalar
        def _(act):
            for m in range(NW):
                proj.split_w_hi(act, 0, m, True)
            for c in range(KC):
                proj.split_x_hi(act, 0, c)

            def group(j, first):
                for k in range(NJOB):
                    proj.take_hi(act, j, k, k % BANKS, first)
                    if k >= NJOB - NW:
                        proj.split_w_hi(act, j + 1, k - (NJOB - NW), False)
            group(0, True)
            act.wait_ge(wo_in, 16)
            nc.scalar.activation(wo_hi[:], wo_raw[:], ACT.Copy).then_inc(wo_hi_ok, 1)
            with act.Fori(1, NG) as j:
                group(j, False)

        @block.vector
        def _(dve):
            nc.vector.memset(facs[:, 1:2], 4.0 / (XSCALE * XSCALE * GSCALE)).then_inc(facs_ok, 1)
            for c in (0, 1, 2):
                proj.split_x_lo(dve, nc.vector, 0, c, proj.x_lo_dve)
            for k in range(NJOB):
                proj.take_lo(dve, 0, k, k % BANKS)
            dve.wait_ge(wo_hi_ok, 1)
            nc.vector.tensor_tensor(wo_lo[:], wo_raw[:], wo_hi[:].bitcast(F32), ALU.subtract).then_inc(wo_lo_ok, 1)
            with dve.Fori(1, NG) as j:
                w = raw[:, bass.ds((j - 1) % 2 * N, N)]
                for k in range(NJOB):
                    proj.take_lo(dve, j, k, k % BANKS)
                    if k == 1:
                        dve.wait_ge(raw_in, 64 * j)
                        nc.vector.tensor_reduce(part[:], w, axis=AX.X, op=ALU.add, apply_absolute_value=True).then_inc(summed, 1)
                    if k == 4:
                        dve.wait_ge(reduced, j)
                        for n, sign in enumerate((0.5, -0.5)):
                            nc.vector.tensor_scalar(half[:, n:n + 1], sum_bank, sign / (HIDDEN * D), None, ALU.mult).then_inc(halved, 1)
                        dve.wait_ge(halved, 2 * j)
                        nc.vector.tensor_scalar(below[:], w, half[:, 1:2], None, ALU.is_lt).then_inc(compared, 1)
                        nc.vector.tensor_scalar(facs[:, 0:1], half[:, 0:1], 1.0 / XSCALE, None, ALU.mult)
                        dve.wait_ge(facs_ok, j)
                        nc.vector.tensor_tensor(facs[:, 1:2], facs[:, 1:2], half[:, 0:1], ALU.mult).then_inc(facs_ok, 1)
                    if k == 5:
                        dve.wait_ge(compared, j)
                        dve.wait_ge(stored, 32 * j)
                        nc.vector.scalar_tensor_tensor(tern[:], w, half[:, 0:1], below[:], ALU.is_gt,
                                                       ALU.subtract).then_inc(ternary, 1)

        @block.tensor
        def _(pe):
            for x_in in proj.x_in:
                pe.wait_ge(x_in, 16)
            pe.wait_ge(ones_ok, 1)
            for k in range(NJOB):
                if JOBS[k] == ("qk", 0, 0):
                    pe.wait_ge(proj.x_lo_dve, 3)
                    pe.wait_ge(proj.x_lo_pool, 1)
                if k >= BANKS:
                    pe.wait_ge(proj.got_lo, k - BANKS + 1)
                proj.multiply(pe, 0, k, k % BANKS)
            with pe.Fori(1, NG) as j:
                for k in range(NJOB):
                    pe.wait_ge(proj.got_lo, NJOB * j + k - BANKS + 1)
                    proj.multiply(pe, j, k, k % BANKS)
                    if k == 4:
                        pe.wait_ge(summed, j)
                        nc.tensor.matmul(sum_bank, ones[:], part[:], start=True, stop=True).then_inc(reduced, 1)


def attention(nc, ctx, lam, qk, vs, oT, ones, ident, psum, proj, ffn):
    sb, sem = scopes(nc, ctx)
    k_st = sb("k_st", [3 * DH, G, 2, S], F32R)
    q_st = sb("q_st", [3 * DH, G, 2, QB], F32R)
    v_st = sb("v_st", [P, SC, P], F32)
    e = sb("e", [P, 2, 2, S], F32)
    mix = sb("mix", [P, 2, S], F32)
    mixT = sb("mixT", [P, 2, SC, G, P], F32)
    nmax = sb("nmax", [P, 2, 2], F32)
    sums = sb("sums", [P, UNITS, 2], F32)
    rsum = sb("rsum", [P, UNITS], F32)
    rsum2 = sb("rsum2", [P, UNITS], F32)
    coef = sb("coef", [P, UNITS], F32)
    pause = sb("pause", [P, 1], F32)
    nlam = sb("nlam", [P, NSTEP * G], F32)
    nlam4 = sb("nlam4", [P, G], F32)
    lam_raw = sb("lam_raw", [P, H], F32)
    rep = sb("rep", [P, G, DH], F32)
    rT = sb("rT", [P, P], F32)
    o_out = sb("o_out", [P, 2, P], F32)

    score_bank = [psum[:, 2 * a:2 * a + 2, :] for a in range(2)]
    flip_bank = [psum[:, 4 + i, :] for i in range(2)]
    pv_bank = psum[:, SIDE, 0:P]
    r_bank = psum[:, SIDE, P:2 * P]

    stack_in = [sem(f"a_stack_in{h}") for h in range(G)]
    scored = [sem(f"a_scored{a}") for a in range(2)]
    maxed = [sem(f"a_maxed{a}") for a in range(2)]
    exped = [sem(f"a_exped{a}") for a in range(2)]
    stored = [sem(f"a_stored{i}") for i in range(2)]
    (v_in, pool_weighed, pool_combined, inverted, inverted2, weighted, combined, flipped, evacuated, pv_done, rep_ready, rep_flipped, rT_ready, o_ready,
     lam_in, lam_step) = (sem("a_" + n) for n in (
         "v_in", "pool_weighed", "pool_combined", "inverted", "inverted2", "weighted", "combined", "flipped", "evacuated", "pv_done", "rep_ready",
         "rep_flipped", "rT_ready", "o_ready", "lam_in", "lam_step"))

    def is_first(i):
        return isinstance(i, int) and i == 0

    def load_stack(sp, i, h):
        b, tb, g = i // (NQB * NG), (i // NG) % NQB, i % NG
        for stack, kind, parts, tokens in ((q_st, 0, (0, 0, 1), bass.ds(tb * QB, QB)), (k_st, 1, (0, 1, 0), slice(0, S))):
            for slot, part in enumerate(parts):
                src = qk[bass.ds(b, 1), kind::2, part, bass.ds(g * P + h * DH, DH), tokens]
                sp.dma_start(stack[slot * DH:(slot + 1) * DH, h, :, :].bitcast(F32),
                             src.rearrange("b a f t -> f (b a) t")).then_inc(stack_in[h], 16)

    def load_v(sp, i):
        if not is_first(i):
            sp.wait_ge(pv_done, QT * i)
        b, g = i // (NQB * NG), i % NG
        sp.dma_start(v_st[:], vs[bass.ds(b, 1), :, bass.ds(g * P, P)].rearrange("a (c p) f -> p (a c) f", p=P)).then_inc(v_in, 16)

    def store_o(sp, i, q):
        sp.wait_ge(o_ready, QT * i + q + 1)
        dst = oT[bass.ds((i % NG) * P, P), bass.ds((i // NG) * QB + q * P, P)]
        sp.dma_start(dst, o_out[:, q % 2, :]).then_inc(stored[q % 2], 16)

    def exponentials(act, i, u, a):
        n = UNITS * i + u
        act.wait_ge(maxed[a], n + 1)
        if not (is_first(i) and u < 2):
            act.wait_ge(combined, n - 1)
            act.wait_ge(pool_combined, n - 1)
        nc.scalar.activation(e[:, a, u % 2, :], score_bank[a].rearrange("p b k -> p (b k)"), ACT.Exp,
                             bias=nmax[:, a, u % 2:u % 2 + 1], accum_out=sums[:, u, a:a + 1]).then_inc(exped[a], 1)

    def evacuate(act, i, u, t):
        if is_first(i) and u < 2:
            return
        m = (u - 2) % UNITS
        q, h = divmod(m, G)
        n = UNITS * i + u - 2
        if t == 0 and h == 0 and not (is_first(i) and m < 2 * G):
            act.wait_ge(pv_done, QT * i + q - 1)
        act.wait_ge(flipped, 2 * n + t + 1)
        nc.scalar.activation(mixT[:, q % 2, t * 4:t * 4 + 4, h, :],
                             flip_bank[t].rearrange("p (c q) -> p c q", q=P), ACT.Copy).then_inc(evacuated, 1)

    def take_r(act, qn, first):
        act.wait_ge(rep_flipped, qn + 1)
        if not first:
            act.wait_ge(o_ready, qn)
        nc.scalar.activation(rT[:], r_bank, ACT.Copy).then_inc(rT_ready, 1)

    def maximum(dve, i, u, a):
        dve.wait_ge(scored[a], UNITS * i + u + 1)
        nc.vector.tensor_reduce(nmax[:, a, u % 2:u % 2 + 1], score_bank[a], axis=AX.XY, op=ALU.max,
                                negate=True).then_inc(maxed[a], 1)

    def invert(dve, i, u):
        if is_first(i) and u == 0:
            return
        m = (u - 1) % UNITS
        n = UNITS * i + u - 1
        if m == 0:
            dve.wait_ge(lam_step, i + 2)
        for a in range(2):
            dve.wait_ge(exped[a], n + 1)
        nc.vector.reciprocal(rsum2[:, m:m + 1], sums[:, m, 1:2]).then_inc(inverted2, 1)

    def weigh(dve, i, u):
        if is_first(i) and u == 0:
            return
        m = (u - 1) % UNITS
        n = UNITS * i + u - 1
        dve.wait_ge(inverted2, n + 1)
        nc.vector.scalar_tensor_tensor(coef[:, m:m + 1], sums[:, m, 0:1], nlam4[:, m % G:m % G + 1], rsum2[:, m:m + 1],
                                       ALU.mult, ALU.mult).then_inc(weighted, 1)
        if m % G == G - 1:
            nc.vector.reciprocal(rsum[:, m - G + 1:m + 1], sums[:, m - G + 1:m + 1, 0]).then_inc(inverted, 1)

    def combine(dve, i, u):
        if is_first(i) and u == 0:
            return
        m = (u - 1) % UNITS
        n = UNITS * i + u - 1
        dve.wait_ge(weighted, n + 1)
        if not (is_first(i) and u < 3):
            dve.wait_ge(flipped, 2 * (n - 1))
        nc.vector.scalar_tensor_tensor(mix[:, m % 2, 0:VW], e[:, 1, m % 2, 0:VW], coef[:, m:m + 1], e[:, 0, m % 2, 0:VW],
                                       ALU.mult, ALU.add).then_inc(combined, 1)

    def pool_combine(pool, i, u):
        if is_first(i) and u == 0:
            return
        m = (u - 1) % UNITS
        n = UNITS * i + u - 1
        pool.wait_ge(weighted, n + 1)
        if not (is_first(i) and u < 3):
            pool.wait_ge(flipped, 2 * (n - 1))
        nc.gpsimd.tensor_tensor(pause[:], ones[:, 0:1], ones[:, 0:1], ALU.mult)
        nc.gpsimd.tensor_scalar(mix[:, m % 2, VW:S], e[:, 1, m % 2, VW:S], coef[:, m:m + 1], 1.0, ALU.mult,
                                ALU.mult).then_inc(pool_weighed, 1)
        pool.wait_ge(pool_weighed, n + 1)
        nc.gpsimd.tensor_tensor(mix[:, m % 2, VW:S], mix[:, m % 2, VW:S], e[:, 0, m % 2, VW:S], ALU.add).then_inc(pool_combined, 1)

    def scale_o(dve, i, q, qn):
        dve.wait_ge(pv_done, qn + 1)
        dve.wait_ge(rT_ready, qn + 1)
        if not (is_first(i) and q < 2):
            dve.wait_ge(stored[q % 2], 16 * (QT // 2) * (i if q < 3 else i - 1) + 16 * (q // 2))
        nc.vector.tensor_tensor(o_out[:, q % 2, :], pv_bank, rT[:], ALU.mult).then_inc(o_ready, 1)

    def replicate(pool, qn, q):
        pool.wait_ge(inverted, qn + 1)
        if not (isinstance(qn, int) and qn == 0):
            pool.wait_ge(rep_flipped, qn)
        nc.gpsimd.tensor_tensor(rep[:], rsum[:, q * G:(q + 1) * G].unsqueeze(2).to_broadcast([P, G, DH]),
                                ones[:].rearrange("p (h d) -> p h d", d=DH), ALU.mult).then_inc(rep_ready, 1)

    def scores(pe, i, u, a):
        q, h = divmod(u, G)
        n = UNITS * i + u
        if q == 0 and a == 0:
            pe.wait_ge(stack_in[h], 16 * 6 * i + 16 * 6)
        if not (is_first(i) and u == 0):
            pe.wait_ge(exped[a], n)
        for kb in range(S // 512):
            last = nc.tensor.matmul(score_bank[a][:, kb, :], q_st[:, h, a, q * P:(q + 1) * P],
                                    k_st[:, h, a, kb * 512:(kb + 1) * 512], start=True, stop=True)
        last.then_inc(scored[a], 1)

    def flip(pe, i, u, t):
        if is_first(i) and u < 2:
            return
        m = (u - 2) % UNITS
        n = UNITS * i + u - 2
        pe.wait_ge((combined, pool_combined)[t], n + 1)
        if not (is_first(i) and u == 2):
            pe.wait_ge(evacuated, 2 * (n - 1) + t + 1)
        for c in range(4):
            last = nc.tensor.transpose(flip_bank[t][:, c * P:(c + 1) * P],
                                       mix[:, m % 2, (4 * t + c) * P:(4 * t + c + 1) * P], ident[:])
        last.then_inc(flipped, 1)

    def values(pe, qn, q, i, half):
        if half == 0:
            pe.wait_ge(evacuated, 2 * G * (qn + 1))
            pe.wait_ge(v_in, 16 * i + 16)
        for c in range(half * SC // 2, (half + 1) * SC // 2):
            for h in range(G):
                last = nc.tensor.matmul(pv_bank[h * DH:(h + 1) * DH, :], v_st[:, c, h * DH:(h + 1) * DH],
                                        mixT[:, q % 2, c, h, :], start=c == 0, stop=c == SC - 1)
        if half:
            last.then_inc(pv_done, 1)
            pe.wait_ge(rep_ready, qn + 1)
            nc.tensor.transpose(r_bank, rep[:].rearrange("p h d -> p (h d)"), ident[:]).then_inc(rep_flipped, 1)

    def is_last_group(i):
        return isinstance(i, int) and i == NG - 1

    def is_tile_first(i):
        return isinstance(i, int) and i == F0

    def late(i):
        return 1 if is_tile_first(i) else 0

    def pv_slots(i):
        return {u + (late(i) if q == 3 else 0): q for u, q in PV_SLOT.items()}

    def values_job(pe, i, u, side, half):
        q = pv_slots(i)[u]
        if q == 3 and is_first(i):
            return
        if half == 0:
            if side == "project" and u > 2:
                pe.wait_ge(proj.got_lo, NJOB * (i + NG) + JOB_SLOT[u - 2] + 1)
            elif side == "feed" and u < 6:
                pe.wait_ge(ffn.step1, 2 * (i - F0) + 1)
            elif side == "feed" and u > 6:
                pe.wait_ge(ffn.gate_ok, GATES * (i - F0) + GATE_SLOT[u - 2] + 1)
            elif side == "feed":
                pe.wait_ge(o_ready, QT * i)
            else:
                pe.wait_ge(o_ready, QT * i - 1)
        if q == 3:
            values(pe, QT * i - 1, 3, i - 1, half)
        else:
            values(pe, QT * i + q, q, i, half)

    def projection_job(pe, i, u, half):
        k = JOB_SLOT[u]
        if half == 0:
            if u % 2 == 0 and not (is_first(i) and u == 4):
                pe.wait_ge(o_ready, QT * i + u // 4 - 1)
            pe.wait_ge(proj.got_lo, NJOB * (i + NG) + sum(v <= u - 2 for v in JOB_SLOT))
            if is_first(i) and k == 0:
                for x_in in proj.x_in:
                    pe.wait_ge(x_in, 32)
            if is_first(i) and k == 2:
                pe.wait_ge(proj.x_lo_dve, 5)
                pe.wait_ge(proj.x_lo_pool, 3)
        proj.multiply(pe, i + NG, k, SIDE + u % 2, (half,))

    def feed_job(pe, i, u, half):
        t = i - F0
        if u == late(i):
            if half == 0:
                pe.wait_ge(o_ready, QT * i - 1)
                if is_tile_first(i):
                    pe.wait_ge(proj.got_lo, 2 * NG * NJOB)
                    pe.wait_ge(ffn.wo_in, 32)
            ffn.project(pe, t, SIDE, half)
        if u == 3 + late(i) and half == 0:
            if not is_tile_first(i):
                pe.wait_ge(ffn.step2, 2 * (t - 1) + 1)
            ffn.flip(pe, t, SIDE + 1)
        if u in GATE_SLOT:
            if half == 0:
                g = sum(v <= u - 2 for v in GATE_SLOT)
                if g:
                    pe.wait_ge(ffn.gate_ok, GATES * t + g)
                elif is_tile_first(i):
                    pe.wait_ge(ffn.w13_in, 32)
                if u % 2 == 0:
                    pe.wait_ge(o_ready, QT * i + u // 4 - 1)
            ffn.hidden_pair(pe, t, GATE_SLOT[u], SIDE + u % 2, half)
        if u == 13 and half == 0:
            pe.wait_ge(ffn.gate_ok, GATES * t + GATE_SLOT[u - 2] + 1)
            if is_tile_first(i):
                pe.wait_ge(ffn.w2_in, 16)
        if u in (13, 15):
            ffn.back(pe, t, SIDE + 1, u - 13 + half)

    def side_job(pe, i, u, side, half):
        if u in pv_slots(i):
            values_job(pe, i, u, side, half)
        if side == "project" and u in JOB_SLOT:
            projection_job(pe, i, u, half)
        if side == "feed":
            feed_job(pe, i, u, half)

    def tensor_step(pe, i, side):
        for u in range(UNITS):
            scores(pe, i, u, 0)
            flip(pe, i, u, 0)
            scores(pe, i, u, 1)
            flip(pe, i, u, 1)
            side_job(pe, i, u, side, 0)
            side_job(pe, i, u, side, 1)

    def scalar_step(act, i, side):
        for u in range(UNITS):
            if u - 1 in pv_slots(i):
                q = pv_slots(i)[u - 1]
                if q < 3:
                    take_r(act, QT * i + q, is_first(i) and q == 0)
                elif not is_first(i):
                    take_r(act, QT * i - 1, False)
            if side == "project":
                if is_first(i) and u in (3, 4):
                    for c in (2 * u - 6, 2 * u - 5):
                        proj.split_x_hi(act, 1, c)
                if u - 1 in JOB_SLOT:
                    k = JOB_SLOT[u - 1]
                    proj.take_hi(act, i + NG, k, SIDE + (u - 1) % 2, False)
                    if k >= NJOB - NW and not is_last_group(i):
                        proj.split_w_hi(act, i + NG + 1, k - (NJOB - NW), False)
            if side == "feed":
                t = i - F0
                if u == 1 and is_tile_first(i):
                    ffn.split_hi(act, 0)
                if u == UNITS - 1:
                    ffn.split_hi(act, t + 1)
                if u == 4 + late(i):
                    ffn.y_parts_hi(act, t, SIDE + 1)
                if u - 1 in GATE_SLOT:
                    ffn.tanh(act, t, GATE_SLOT[u - 1], SIDE + (u - 1) % 2)
                if u - 2 in GATE_SLOT:
                    ffn.gate_hi(act, t, GATE_SLOT[u - 2])
            for half in range(2):
                exponentials(act, i, u, half)
                evacuate(act, i, u, half)
        if side == "project":
            proj.take_hi(act, i + NG, NJOB - 1, SIDE + 1, False)
            if not is_last_group(i):
                proj.split_w_hi(act, i + NG + 1, NW - 1, False)

    def vector_step(dve, i, side):
        t = i - F0
        for u in range(UNITS):
            gate = GATE_SLOT.get(u - 1) if side == "feed" else None
            q = pv_slots(i).get(u - 1)
            maximum(dve, i, u, 0)
            invert(dve, i, u)
            if gate is not None:
                ffn.gate(dve, t, gate, SIDE + (u - 1) % 2)
            elif q is not None and q < 3:
                scale_o(dve, i, q, QT * i + q)
            elif q == 3 and not is_first(i):
                scale_o(dve, i, q, QT * i - 1)
            weigh(dve, i, u)
            if gate is not None:
                ffn.gate2(dve, t, gate, SIDE + (u - 1) % 2)
            maximum(dve, i, u, 1)
            combine(dve, i, u)
            if side == "project":
                if is_first(i) and u in (3, 4):
                    proj.split_x_lo(dve, nc.vector, 1, u - 3, proj.x_lo_dve)
                if u - 1 in JOB_SLOT:
                    proj.take_lo(dve, i + NG, JOB_SLOT[u - 1], SIDE + (u - 1) % 2)
            if side == "feed":
                if u == 0 and not is_tile_first(i):
                    ffn.residual2(dve, t - 1, SIDE + 1)
                if u == 1 + late(i):
                    ffn.residual(dve, t, SIDE)
                if u == 2 + late(i):
                    ffn.norm1(dve, t)
                if u == 3 and not is_tile_first(i):
                    ffn.norm2(dve, t - 1)
                if u == 4 + late(i):
                    ffn.y_parts_lo(dve, t, SIDE + 1)
        if side == "project":
            proj.take_lo(dve, i + NG, NJOB - 1, SIDE + 1)

    def gpsimd_step(pool, i, side):
        pool_combine(pool, i, 0)
        if not is_first(i):
            pool.wait_ge(weighted, UNITS * i)
        nc.gpsimd.tensor_tensor(nlam4[:], nlam[:, bass.ds(i * G, G)], ones[:, 0:G], ALU.mult).then_inc(lam_step, 1)
        if not is_first(i):
            replicate(pool, QT * i - 1, 3)
        for u in range(UNITS):
            if u:
                pool_combine(pool, i, u)
            if u == 1 and is_tile_first(i):
                pool.wait_ge(ffn.x_in, 32)
                nc.gpsimd.memset(ffn.expo[:], -0.5).then_inc(ffn.expo_ok, 1)
                nc.gpsimd.memset(ffn.eps[:], EPS).then_inc(ffn.expo_ok, 1)
                for s in proj.stored:
                    pool.wait_ge(s, 2 * NG * NJOB * 16)
                ffn.split_lo(pool, 0)
                pool.wait_ge(ffn.expo_ok, 2)
            if side == "project":
                if is_first(i) and u in (3, 4):
                    proj.split_x_lo(pool, nc.gpsimd, 1, u - 1, proj.x_lo_pool)
                if u - 1 in JOB_SLOT and JOB_SLOT[u - 1] >= NJOB - MATS and not is_last_group(i):
                    proj.split_w_lo(pool, i + NG + 1, JOB_SLOT[u - 1] - (NJOB - MATS))
                if u == 3 and not is_first(i):
                    proj.split_w_lo(pool, i + NG, MATS - 1)
            if u and u % G == 0:
                replicate(pool, QT * i + u // G - 1, u // G - 1)
            if side == "feed":
                t = i - F0
                if u == 0 and not is_tile_first(i):
                    ffn.power(pool, t - 1, 1, ffn.stat2, ffn.pow2, 2 * t)
                if u == 1 + late(i):
                    ffn.power(pool, t, 0, ffn.stat1, ffn.pow1, 2 * t + 1)
                if u - 2 in GATE_SLOT:
                    ffn.gate_lo(pool, t, GATE_SLOT[u - 2])
                if u == UNITS - 1:
                    ffn.split_lo(pool, t + 1)

    def sync_step(sp, i, side, last=False):
        if side == "feed" and is_tile_first(i):
            sp.wait_ge(proj.product, 2 * NG * NJOB)
            sp.wait_ge(proj.w_lo_ok, 2 * NG * MATS)
            sp.wait_ge(proj.got_lo, 2 * NG * NJOB)
            ffn.load(sp, 0)
            ffn.load_weights(sp)
        for u in range(UNITS):
            if u - 1 in pv_slots(i):
                q = pv_slots(i)[u - 1]
                if q < 3:
                    store_o(sp, i, q)
                elif not is_first(i):
                    store_o(sp, i - 1, 3)
                if q == 3:
                    load_v(sp, i)
                    if side == "feed" and not is_tile_first(i):
                        ffn.store(sp, i - F0 - 1)
            if side == "project" and u == 7 and is_last_group(i):
                sp.wait_ge(proj.product, (2 * NG - 1) * NJOB + 2)
                ffn.load_wo(sp)
            if side == "project" and u == 4 and not is_last_group(i):
                proj.load_w(sp, i + NG + 1, False)
            if side == "project" and u - 2 in JOB_SLOT:
                proj.store(sp, i + NG, 1, JOB_SLOT[u - 2])
            if side == "feed" and u == 10:
                if not is_tile_first(i):
                    sp.wait_ge(ffn.stored, 16 * (i - F0))
                sp.wait_ge(ffn.step1, 2 * (i - F0) + 1)
                sp.wait_ge(stored[0], 16 * 2 * i + 16)
                sp.wait_ge(stored[1], 16 * 2 * i)
                ffn.load(sp, i - F0 + 1)
            if u >= UNITS - G + 1 and not last:
                h = u - (UNITS - G + 1)
                sp.wait_ge(scored[1], UNITS * i + UNITS - G + h + 1)
                load_stack(sp, i + 1, h)
        if side == "project":
            proj.store(sp, i + NG, 1, NJOB - 1)
        if not last:
            sp.wait_ge(scored[1], UNITS * i + UNITS)
            load_stack(sp, i + 1, G - 1)

    def every_step(eng, step):
        step(eng, 0, "project")
        with eng.Fori(1, NG - 1) as i:
            step(eng, i, "project")
        step(eng, NG - 1, "project")
        step(eng, F0, "feed")
        with eng.Fori(F0 + 1, NSTEP) as i:
            step(eng, i, "feed")

    QL = QT * NSTEP - 1
    TL = NTILE - 1

    with nc.Block() as block:
        @block.sync
        def _(sp):
            sp.dma_start(lam_raw[:], lam.partition_broadcast(P)).then_inc(lam_in, 16)
            for s in proj.stored:
                sp.wait_ge(s, NG * NJOB * 16)
            for h in range(G):
                load_stack(sp, 0, h)
            proj.load_x(sp, 1)
            sync_step(sp, 0, "project")
            with sp.Fori(1, NG - 1) as i:
                sync_step(sp, i, "project")
            sync_step(sp, NG - 1, "project")
            sync_step(sp, F0, "feed")
            with sp.Fori(F0 + 1, NSTEP - 1) as i:
                sync_step(sp, i, "feed")
            sync_step(sp, NSTEP - 1, "feed", last=True)
            store_o(sp, NSTEP - 1, 3)
            ffn.store(sp, TL)
            sp.wait_ge(ffn.stored, 16 * NTILE)
            for half in range(2):
                sp.wait_ge(stored[half], 16 * 2 * NSTEP)
            sp.wait_ge(ffn.x_in, 32 * (NTILE + 1))

        @block.gpsimd
        def _(pool):
            pool.wait_ge(lam_in, 16)
            for r in range(NSTEP * G // H):
                last = nc.gpsimd.tensor_scalar(nlam[:, r * H:(r + 1) * H], lam_raw[:], -1.0, 1.0, ALU.mult, ALU.mult)
            last.then_inc(lam_step, 1)
            pool.wait_ge(lam_step, 1)
            every_step(pool, gpsimd_step)
            pool_combine(pool, NSTEP, 0)
            replicate(pool, QL, 3)
            ffn.power(pool, TL, 1, ffn.stat2, ffn.pow2, 2 * TL + 2)

        @block.scalar
        def _(act):
            every_step(act, scalar_step)
            for u in range(2):
                for half in range(2):
                    evacuate(act, NSTEP, u, half)
            take_r(act, QL, False)

        @block.vector
        def _(dve):
            every_step(dve, vector_step)
            invert(dve, NSTEP, 0)
            weigh(dve, NSTEP, 0)
            combine(dve, NSTEP, 0)
            scale_o(dve, NSTEP, 3, QL)
            ffn.residual2(dve, TL, SIDE + 1)
            ffn.norm2(dve, TL)

        @block.tensor
        def _(pe):
            every_step(pe, tensor_step)
            for u in range(2):
                for half in range(2):
                    flip(pe, NSTEP, u, half)
            pe.wait_ge(o_ready, QL)
            for half in range(2):
                values(pe, QL, 3, NSTEP - 1, half)


def last_block(nc, ctx, x, oT, ffn, facs, ident, out, psum):
    w13, w2, wo_hi, wo_lo = ffn.w13, ffn.w2, ffn.wo_hi, ffn.wo_lo
    sb, sem = scopes(nc, ctx)
    TT = QB // P
    T0 = T - QB
    o_raw = sb("l_o_raw", [P, KC, QB], F32)
    o_hi = sb("l_o_hi", [P, KC, QB], F32R)
    o_lo = sb("l_o_lo", [P, KC, QB], F32R)
    res = sb("l_res", [P, TT, D], F32)
    y = sb("l_y", [P, TT, D], F32)
    z = sb("l_z", [P, TT, D], F32)
    stats = sb("l_stats", [P, TT, 6], F32)
    pause = sb("l_pause", [P, 1], F32)
    mv = sb("l_mv", [P, 2, TT, 2], F32)
    rstd = sb("l_rstd", [P, 2, TT], F32)
    consts = sb("l_consts", [P, 1], F32)
    y_hi = sb("l_y_hi", [P, KC, QB], F16)
    y_lo = sb("l_y_lo", [P, KC, QB], F16)
    th = sb("l_th", [P, 2, QB], F32)
    gated = sb("l_gated", [P, 2, QB], F32)
    g_hi = sb("l_g_hi", [P, FC, QB], F16)
    g_lo = sb("l_g_lo", [P, FC, QB], F16)
    (x_in, o_hi_ok, o_lo_ok, projected, stat, powed, normed, dve_step, flipped, y_hi_ok, y_lo_ok,
     hidden, tanhed, gate_ok, g_hi_ok, g_lo_ok, down, stored, const_ok, hidden_used) = (sem("l_" + n) for n in (
         "x_in", "o_hi_ok", "o_lo_ok", "projected", "stat", "powed", "normed", "dve_step",
         "flipped", "y_hi_ok", "y_lo_ok", "hidden", "tanhed", "gate_ok", "g_hi_ok", "g_lo_ok", "down", "stored", "const_ok", "hidden_used"))

    o_in = [sem(f"l_o_in{c}") for c in range(KC)]

    with nc.Block() as block:
        @block.sync
        def _(sp):
            for c in range(KC):
                sp.dma_start(o_raw[:, c, :], oT[c * P:(c + 1) * P, T0:T]).then_inc(o_in[c], 16)
            sp.dma_start(res[:], x[T0:T, :].rearrange("(c p) d -> p c d", p=P)).then_inc(x_in, 16)
            for tt in range(TT):
                sp.wait_ge(normed, TT + tt + 1)
                sp.dma_start(out[T0 + tt * P:T0 + (tt + 1) * P, :], z[:, tt, :]).then_inc(stored, 16)
            sp.wait_ge(stored, 16 * TT)

        @block.gpsimd
        def _(pool):
            nc.gpsimd.memset(consts[:], -0.5).then_inc(const_ok, 1)
            pool.wait_ge(const_ok, 1)
            for ln in range(2):
                for tt in range(TT):
                    pool.wait_ge(stat, TT * ln + tt + 1)
                    nc.gpsimd.tensor_tensor(rstd[:, ln, tt:tt + 1], mv[:, ln, tt, 1:2], consts[:], ALU.pow).then_inc(powed, 1)
                if ln == 0:
                    for f in range(FC):
                        pool.wait_ge(g_hi_ok, f + 1)
                        nc.gpsimd.tensor_tensor(g_lo[:, f, :], gated[:, f % 2, :], g_hi[:, f, :], ALU.subtract).then_inc(g_lo_ok, 1)

        def gate_copy(act, f):
            act.wait_ge(gate_ok, f + 1)
            nc.scalar.activation(g_hi[:, f, :], gated[:, f % 2, :], ACT.Copy).then_inc(g_hi_ok, 1)

        @block.scalar
        def _(act):
            for c in range(KC):
                act.wait_ge(o_in[c], 16)
                nc.scalar.activation(o_hi[:, c, :], o_raw[:, c, :], ACT.Copy).then_inc(o_hi_ok, 1)
            for c in range(KC):
                act.wait_ge(flipped, c + 1)
                nc.scalar.activation(y_hi[:, c, :], psum[:, c % 2, :], ACT.Copy, scale=XSCALE).then_inc(y_hi_ok, 1)
            for f in range(FC):
                act.wait_ge(hidden, 2 * f + 1)
                if f >= 2:
                    act.wait_ge(gate_ok, f - 1)
                nc.scalar.activation(th[:, f % 2, :], psum[:, 2 + 2 * (f % 2), :], ACT.Tanh, scale=facs[:, 0:1]).then_inc(tanhed, 1)
                if f >= 1:
                    gate_copy(act, f - 1)
            gate_copy(act, FC - 1)

        @block.vector
        def _(dve):
            def moments(ln, tt, base):
                dve.wait_ge(dve_step, base + 1)
                nc.vector.bn_stats(stats[:, tt, :], z[:, tt, :]).then_inc(dve_step, 1)
                dve.wait_ge(dve_step, base + 2)
                nc.vector.memset(pause[:], 0.0)
                nc.vector.bn_aggr(mv[:, ln, tt, :], stats[:, tt, :]).then_inc(dve_step, 1)
                dve.wait_ge(dve_step, base + 3)
                nc.vector.tensor_scalar(mv[:, ln, tt, 1:2], mv[:, ln, tt, 1:2], EPS, None, ALU.add).then_inc(stat, 1)

            def normalise(ln, tt, dst, count):
                dve.wait_ge(powed, count)
                nc.vector.tensor_scalar(dst, z[:, tt, :], mv[:, ln, tt, 0:1], rstd[:, ln, tt:tt + 1], ALU.subtract,
                                        ALU.mult).then_inc(normed, 1)
            for c in range(KC):
                dve.wait_ge(o_hi_ok, c + 1)
                nc.vector.tensor_tensor(o_lo[:, c, :], o_raw[:, c, :], o_hi[:, c, :].bitcast(F32), ALU.subtract).then_inc(o_lo_ok, 1)
            dve.wait_ge(x_in, 16)
            for tt in range(TT):
                dve.wait_ge(projected, tt + 1)
                nc.vector.tensor_tensor(z[:, tt, :], psum[:, 6 + tt % 2, :], res[:, tt, :], ALU.add).then_inc(dve_step, 1)
                moments(0, tt, 3 * tt)
                if tt:
                    normalise(0, tt - 1, y[:, tt - 1, :], tt)
            normalise(0, TT - 1, y[:, TT - 1, :], TT)
            for c in range(KC):
                dve.wait_ge(y_hi_ok, c + 1)
                nc.vector.scalar_tensor_tensor(y_lo[:, c, :], psum[:, c % 2, :], XSCALE, y_hi[:, c, :], ALU.mult,
                                               ALU.subtract).then_inc(y_lo_ok, 1)
            for f in range(FC):
                dve.wait_ge(tanhed, f + 1)
                if f >= 2:
                    dve.wait_ge(g_lo_ok, f - 1)
                nc.vector.scalar_tensor_tensor(gated[:, f % 2, :], th[:, f % 2, :], 1.0, psum[:, 2 + 2 * (f % 2), :],
                                               ALU.add, ALU.mult).then_inc(hidden_used, 1)
                dve.wait_ge(hidden, 2 * f + 2)
                dve.wait_ge(hidden_used, f + 1)
                nc.vector.scalar_tensor_tensor(gated[:, f % 2, :], gated[:, f % 2, :], GSCALE, psum[:, 3 + 2 * (f % 2), :],
                                               ALU.mult, ALU.mult).then_inc(gate_ok, 1)
            for tt in range(TT):
                dve.wait_ge(down, tt + 1)
                nc.vector.scalar_tensor_tensor(z[:, tt, :], psum[:, 6 + tt % 2, :], facs[:, 1:2], y[:, tt, :], ALU.mult,
                                               ALU.add).then_inc(dve_step, 1)
                moments(1, tt, 3 * (TT + tt))
                if tt:
                    normalise(1, tt - 1, z[:, tt - 1, :], TT + tt)
            normalise(1, TT - 1, z[:, TT - 1, :], 2 * TT)

        @block.tensor
        def _(pe):
            pe.wait_ge(o_hi_ok, KC)
            for tt in range(TT):
                if tt >= 2:
                    pe.wait_ge(dve_step, 3 * (tt - 2) + 1)
                n = 0
                for op, wp in ((o_hi, wo_hi), (o_hi, wo_lo), (o_lo, wo_hi)):
                    if tt == 0 and op is o_lo:
                        pe.wait_ge(o_lo_ok, KC)
                    for c in range(KC):
                        last = nc.tensor.matmul(psum[:, 6 + tt % 2, :], op[:, c, tt * P:(tt + 1) * P], wp[:, c, :],
                                                start=n == 0, stop=n == 3 * KC - 1)
                        n += 1
                last.then_inc(projected, 1)
            pe.wait_ge(normed, TT)
            for c in range(KC):
                if c >= 2:
                    pe.wait_ge(y_lo_ok, c - 1)
                for tt in range(TT):
                    last = nc.tensor.transpose(psum[:, c % 2, tt * P:(tt + 1) * P], y[:, tt, c * P:(c + 1) * P], ident[:])
                last.then_inc(flipped, 1)
            pe.wait_ge(y_lo_ok, KC)
            for f in range(FC):
                if f >= 2:
                    pe.wait_ge(gate_ok, f - 1)
                for m in range(2):
                    n = 0
                    for part in (y_hi, y_lo):
                        for c in range(KC):
                            last = nc.tensor.matmul(psum[:, 2 + m + 2 * (f % 2), :], w13[:, m, c, f * P:(f + 1) * P],
                                                    part[:, c, :], start=n == 0, stop=n == 2 * KC - 1)
                            n += 1
                    last.then_inc(hidden, 1)
            pe.wait_ge(g_lo_ok, FC)
            for tt in range(TT):
                if tt >= 2:
                    pe.wait_ge(dve_step, 3 * (TT + tt - 2) + 1)
                n = 0
                for part in (g_hi, g_lo):
                    for f in range(FC):
                        last = nc.tensor.matmul(psum[:, 6 + tt % 2, :], part[:, f, tt * P:(tt + 1) * P], w2[:, f, :],
                                                start=n == 0, stop=n == 2 * FC - 1)
                        n += 1
                last.then_inc(down, 1)


def build(nc, x, xT, w5, woT, lam, wff, out):
    qk = nc.dram_tensor("qk_parts", [B, MATS, 2, D, S], F32, kind="Internal").ap()
    vs = nc.dram_tensor("v_rows", [B, S, D], F32, kind="Internal").ap()
    oT = nc.dram_tensor("o_T", [D, T], F32, kind="Internal").ap()
    wq = nc.dram_tensor("w_ternary", [3, P, KC * HP], F16, kind="Internal").ap()
    wod = nc.dram_tensor("wo_parts", [2, P, KC * D], F32, kind="Internal").ap()
    with ExitStack() as whole:
        sb, sem = scopes(nc, whole)
        psum = whole.enter_context(nc.psum_tensor("psum", [P, 8, 512], F32))
        facs = sb("facs", [P, 2], F32)
        ident = sb("ident", [P, P], F32)
        ones = sb("ones", [P, P], F32)
        id_ok = sem("id_ok")
        with nc.Block() as block:
            @block.gpsimd
            def _(pool):
                nc.gpsimd.memset(ident[:], 0.0).then_inc(id_ok, 1)
                pool.wait_ge(id_ok, 1)
                nc.gpsimd.affine_select(out=ident[:], in_=ident[:], compare_op=ALU.not_equal, fill=1.0, base=0,
                                        pattern=[[-1, P]], channel_multiplier=1).then_inc(id_ok, 1)
        sems = whole.enter_context(ExitStack())
        with ExitStack() as region:
            proj = Projections(nc, region, sems, xT, w5, qk, vs, psum)
            with ExitStack() as ctx:
                prepare(nc, ctx, proj, wff, woT, wq, wod, facs, ones)
        with ExitStack() as region:
            ffn = FeedForward(nc, region, sems, x, oT, wq, wod, facs, ident, out, psum)
            with nc.sbuf_tensor("filler", [P, max(0, proj.size - ffn.size) // 4], F32), ExitStack() as ctx:
                attention(nc, ctx, lam, qk, vs, oT, ones, ident, psum, proj, ffn)
            with ExitStack() as ctx:
                last_block(nc, ctx, x, oT, ffn, facs, ident, out, psum)


def kernel(**inputs):
    import numpy as np
    import concourse.bacc as bacc
    from concourse.bass_utils import run_bass_kernel_spmd as run

    a = {k.replace("L0_", ""): np.asarray(v) for k, v in inputs.items()}

    def padded(w, shape):
        out = np.zeros(shape, w.dtype)
        out[tuple(slice(0, n) for n in w.shape)] = w
        return out

    def on_partitions(w):
        return w.reshape(-1, P, w.shape[1]).transpose(1, 0, 2).reshape(P, -1)

    wT = np.stack([a[f"attn_{n}_w"].T for n in ("q1", "k1", "q2", "k2", "v")])
    laid = {
        "x": a["attn_x"].reshape(T, D),
        "xT": a["attn_x"].transpose(0, 2, 1),
        "w5": wT.reshape(NW, KC, P, NG, P).transpose(3, 2, 0, 1, 4).reshape(NG, P, NW * KC * P),
        "woT": a["attn_o_w"].T,
        "lam": a["attn_lambda_param"],
        "wff": np.stack([on_partitions(padded(a["ffn_w2"].T, (HP, D))),
                         on_partitions(padded(a["ffn_w3"].T, (D, HP))),
                         on_partitions(padded(a["ffn_w1"].T, (D, HP)))]),
    }
    laid = {k: np.ascontiguousarray(v) for k, v in laid.items()}
    nc = bacc.Bacc("TRN2", target_bir_lowering=False, num_devices=1)
    args = [nc.dram_tensor(f"in_{k}", v.shape, mybir.dt.from_np(v.dtype), kind="ExternalInput").ap() for k, v in laid.items()]
    out = nc.dram_tensor("out", (T, D), F32, kind="ExternalOutput").ap()
    build(nc, *args, out)
    r = run(nc, [{f"in_{k}": v for k, v in laid.items()}], core_ids=[0])
    return r.results[0]["out"].reshape(B, S, D)
```
